# Optimizing a Trainium2 kernel written in Bass

```python
import numpy as np
import jax
import jax.numpy as jnp

def _softmax(x, axis=-1):
    return jax.nn.softmax(x, axis=axis)

def _gelu(x):
    return jax.nn.gelu(x, approximate=True)

def _silu(x):
    return jax.nn.silu(x)

def _sigmoid(x):
    return jax.nn.sigmoid(x)

def _layernorm(x, axis=-1, eps=1e-05):
    m = jnp.mean(x, axis=axis, keepdims=True)
    v = jnp.var(x, axis=axis, keepdims=True)
    return (x - m) / jnp.sqrt(v + eps)

def _scatter_add(tgt, idx, src, axis=0):
    return tgt.at[idx].add(src)

def _segment_sum(src, seg, n):
    return jax.ops.segment_sum(src, seg, n)
kernel_name = 'mk_perceiver_d2_seqx_r8_442a14'

def setup_inputs(seed: int=0):
    np.random.seed(seed)
    _w = jnp.asarray

    def _rec_inputs():
        import jax
        import jax.numpy as jnp
        _rk = jax.random.key(seed)
        x = -0.0005207 + 1.001 * jax.random.normal(jax.random.fold_in(_rk, 1), (64, 32, 512), jnp.float32)
        _lenS = 32 - jax.random.randint(jax.random.fold_in(_rk, 7), (64,), 0, max(1, 32 // 4) + 1, jnp.int32)
        _lenS2 = 257 - jax.random.randint(jax.random.fold_in(_rk, 8), (64,), 0, max(1, 257 // 4) + 1, jnp.int32)
        _ctx_4096P = jax.random.normal(jax.random.fold_in(_rk, 11), (64, 16, 512), jnp.float32)
        _ctx_4096c = jax.random.dirichlet(jax.random.fold_in(_rk, 511), 0.3 * jnp.ones((16,), jnp.float32), (64, 257))
        _ctx_4096t = jnp.einsum('bsk,bkd->bsd', _ctx_4096c, _ctx_4096P)
        _ctx_4096t = _ctx_4096t * jax.lax.rsqrt(jnp.mean(jnp.square(_ctx_4096t)) + 1e-12) * 0.953939
        ctx_4096 = -0.00010331 + 0.999899 * (_ctx_4096t + 0.3 * jax.random.normal(jax.random.fold_in(_rk, 611), (64, 257, 512), jnp.float32))
        return (x, ctx_4096)
    x, ctx_4096 = _rec_inputs()

    def _L0_xattn_setup():
        import jax, jax.numpy as jnp
        import numpy as np
        B, Q, D = (8, 64, 512)
        CTX = 512
        H, KV, HD = (16, 4, 96)
        G = H // KV
        key = jax.random.key(seed)
        ks = jax.random.split(key, 6)
        s = 0.02
        return {'latents': jax.random.normal(ks[0], (B, Q, D), jnp.float32), 'context': jax.random.normal(ks[1], (B, CTX, D), jnp.float32), 'Wq': jax.random.normal(ks[2], (H * HD, D), jnp.float32) * s, 'Wk': jax.random.normal(ks[3], (KV * HD, D), jnp.float32) * s, 'Wv': jax.random.normal(ks[4], (KV * HD, D), jnp.float32) * s, 'Wo': jax.random.normal(ks[5], (D, H * HD), jnp.float32) * s}
    _L0_xattn_all = _L0_xattn_setup()
    _L0_xattn_in = {k: v for k, v in _L0_xattn_all.items() if k in ('Wq', 'Wk', 'Wv', 'Wo')}
    del _L0_xattn_all

    def _L0_attn_setup():
        import jax, jax.numpy as jnp
        import numpy as np
        DIM = 512
        N_HEADS = 32
        N_KV_HEADS = 8
        HEAD_DIM = DIM // N_HEADS
        N_REP = N_HEADS // N_KV_HEADS
        THETA = 10000.0
        B, S = (4, 128)

        def _rope_cos_sin(seq_len):
            freqs = 1.0 / THETA ** (jnp.arange(0, HEAD_DIM, 2, dtype=jnp.float32) / HEAD_DIM)
            t = jnp.arange(seq_len, dtype=jnp.float32)
            ang = jnp.outer(t, freqs)
            return (jnp.cos(ang), jnp.sin(ang))

        def _apply_rope(x, cos, sin):
            xr = x[..., 0::2]
            xi = x[..., 1::2]
            c = cos[None, :, None, :]
            s = sin[None, :, None, :]
            out_r = xr * c - xi * s
            out_i = xr * s + xi * c
            return jnp.stack([out_r, out_i], axis=-1).reshape(x.shape)
        key = jax.random.key(seed)
        ks = jax.random.split(key, 5)
        sc = 1.0 / np.sqrt(DIM).astype(np.float32)
        x = jax.random.normal(ks[0], (B, S, DIM), jnp.float32)
        wq = jax.random.normal(ks[1], (DIM, N_HEADS * HEAD_DIM), jnp.float32) * sc
        wk = jax.random.normal(ks[2], (DIM, N_KV_HEADS * HEAD_DIM), jnp.float32) * sc
        wv = jax.random.normal(ks[3], (DIM, N_KV_HEADS * HEAD_DIM), jnp.float32) * sc
        wo = jax.random.normal(ks[4], (N_HEADS * HEAD_DIM, DIM), jnp.float32) * sc
        return {'x': x, 'wq': wq, 'wk': wk, 'wv': wv, 'wo': wo}
    _L0_attn_all = _L0_attn_setup()
    _L0_attn_in = {k: v for k, v in _L0_attn_all.items() if k in ('wq', 'wk', 'wv', 'wo')}
    del _L0_attn_all

    def _L0_ffn_setup():
        import jax, jax.numpy as jnp
        import numpy as np
        LORA_RANK = 16
        LORA_ALPHA = 16
        LORA_SCALE = LORA_ALPHA / LORA_RANK
        key = jax.random.key(seed)
        k1, k2, k3, k4, k5 = jax.random.split(key, 5)
        B, S, D_IN, D_OUT, N_LORA, R = (8, 256, 512, 512, 3, LORA_RANK)
        std = 1.0 / np.sqrt(D_IN)
        x = jax.random.normal(k1, (B, S, D_IN), dtype=jnp.float32)
        weight = jax.random.truncated_normal(k2, -3.0, 3.0, (D_OUT, D_IN), dtype=jnp.float32) * std
        bias = jax.random.normal(k3, (D_OUT,), dtype=jnp.float32) * 0.01
        lora_A = jax.random.normal(k4, (N_LORA, R, D_IN), dtype=jnp.float32) * std
        lora_B = jax.random.normal(k5, (N_LORA, D_OUT, R), dtype=jnp.float32) * 0.02
        lora_start_indices = jnp.arange(4, dtype=jnp.int64) * 2
        return {'x': x, 'weight': weight, 'bias': bias, 'lora_A': lora_A, 'lora_B': lora_B, 'lora_start_indices': lora_start_indices}
    _L0_ffn_all = _L0_ffn_setup()
    _L0_ffn_in = {k: v for k, v in _L0_ffn_all.items() if k in ('weight', 'bias', 'lora_A', 'lora_B', 'lora_start_indices')}
    del _L0_ffn_all

    def _L1_xattn_setup():
        import jax, jax.numpy as jnp
        import numpy as np
        import math
        EPS = 1e-05
        LAMBDA = 0.6

        def _crucial_k(C):
            f = math.floor(LAMBDA * C)
            return f + f % 2

        def _conv1d(y, w):
            return jax.lax.conv_general_dilated(y, w, window_strides=(1,), padding=((3, 3),), dimension_numbers=('NCH', 'OIH', 'NCH'))

        def _norm_active(z, gamma, beta):
            mu = jnp.mean(z, axis=(0, 2), keepdims=True)
            var = jnp.mean((z - mu) ** 2, axis=(0, 2), keepdims=True)
            zn = (z - mu) * jax.lax.rsqrt(var + EPS)
            zn = zn * gamma.reshape(1, -1, 1) + beta.reshape(1, -1, 1)
            return jax.nn.sigmoid(jax.nn.relu(zn))
        key = jax.random.key(seed)
        k1, k2, k3 = jax.random.split(key, 3)
        B, C, L = (32, 32, 512)
        x = jax.random.normal(k1, (B, C, L), dtype=jnp.float32)
        channel_map = jax.random.normal(k2, (B, C, L), dtype=jnp.float32)
        fan_in = 2 * 7
        bound = 1.0 / math.sqrt(fan_in)
        conv_w = jax.random.uniform(k3, (1, 2, 7), jnp.float32, -bound, bound)
        bn_gamma = jnp.ones((1,), jnp.float32)
        bn_beta = jnp.zeros((1,), jnp.float32)
        return {'x': x, 'channel_map': channel_map, 'conv_w': conv_w, 'bn_gamma': bn_gamma, 'bn_beta': bn_beta}
    _L1_xattn_all = _L1_xattn_setup()
    _L1_xattn_in = {k: v for k, v in _L1_xattn_all.items() if k in ('conv_w', 'bn_gamma', 'bn_beta')}
    del _L1_xattn_all

    def _L1_attn_setup():
        import jax, jax.numpy as jnp
        import numpy as np
        B, S, HIDDEN = (2, 256, 512)
        TP = 2
        PART = HIDDEN // TP
        NUM_HEADS = 16 // TP
        HEAD_DIM = PART // NUM_HEADS
        MASKED_BIAS = -10000.0
        key = jax.random.key(seed)
        k_x, k_wq, k_bq, k_wo, k_bo = jax.random.split(key, 5)
        x = jax.random.normal(k_x, (B, S, HIDDEN), dtype=jnp.float32)
        w_qkv = jax.random.normal(k_wq, (3 * PART, HIDDEN), dtype=jnp.float32) * 0.02
        b_qkv = jax.random.normal(k_bq, (3 * PART,), dtype=jnp.float32) * 0.02
        w_o = jax.random.normal(k_wo, (HIDDEN, PART), dtype=jnp.float32) * 0.02
        b_o = jax.random.normal(k_bo, (HIDDEN,), dtype=jnp.float32) * 0.02
        return {'x': x, 'w_qkv': w_qkv, 'b_qkv': b_qkv, 'w_o': w_o, 'b_o': b_o}
    _L1_attn_all = _L1_attn_setup()
    _L1_attn_in = {k: v for k, v in _L1_attn_all.items() if k in ('w_qkv', 'b_qkv', 'w_o', 'b_o')}
    del _L1_attn_all

    def _L1_ffn_setup():
        import jax, jax.numpy as jnp
        import numpy as np
        HIDDEN = 512
        SPARSITY_RATIO = 0.1
        BLOCK_SIZE = max(1, int(HIDDEN * SPARSITY_RATIO * 2))

        def _block_diag_mask(h: int, block_size: int) -> jnp.ndarray:
            idx = jnp.arange(h) // block_size
            return idx[:, None] == idx[None, :]
        key = jax.random.key(seed)
        kx, kw = jax.random.split(key)
        x = jax.random.normal(kx, (8, 256, HIDDEN), dtype=jnp.float32)
        mask = _block_diag_mask(HIDDEN, BLOCK_SIZE)
        eye = jnp.eye(HIDDEN, dtype=jnp.float32)
        W = eye + 0.1 * jax.random.normal(kw, (HIDDEN, HIDDEN), dtype=jnp.float32)
        W = W * mask.astype(jnp.float32) + eye * (~mask).astype(jnp.float32)
        return {'x': x, 'W': W, 'mask': mask}
    _L1_ffn_all = _L1_ffn_setup()
    _L1_ffn_in = {k: v for k, v in _L1_ffn_all.items() if k in ('W', 'mask')}
    del _L1_ffn_all
    return {'x': x, 'ctx_4096': ctx_4096, 'L0_xattn_Wq': _L0_xattn_in['Wq'], 'L0_xattn_Wk': _L0_xattn_in['Wk'], 'L0_xattn_Wv': _L0_xattn_in['Wv'], 'L0_xattn_Wo': _L0_xattn_in['Wo'], 'L0_attn_wq': _L0_attn_in['wq'], 'L0_attn_wk': _L0_attn_in['wk'], 'L0_attn_wv': _L0_attn_in['wv'], 'L0_attn_wo': _L0_attn_in['wo'], 'L0_ffn_weight': _L0_ffn_in['weight'], 'L0_ffn_bias': _L0_ffn_in['bias'], 'L0_ffn_lora_A': _L0_ffn_in['lora_A'], 'L0_ffn_lora_B': _L0_ffn_in['lora_B'], 'L0_ffn_lora_start_indices': _L0_ffn_in['lora_start_indices'], 'L1_xattn_conv_w': _L1_xattn_in['conv_w'], 'L1_xattn_bn_gamma': _L1_xattn_in['bn_gamma'], 'L1_xattn_bn_beta': _L1_xattn_in['bn_beta'], 'L1_attn_w_qkv': _L1_attn_in['w_qkv'], 'L1_attn_b_qkv': _L1_attn_in['b_qkv'], 'L1_attn_w_o': _L1_attn_in['w_o'], 'L1_attn_b_o': _L1_attn_in['b_o'], 'L1_ffn_W': _L1_ffn_in['W'], 'L1_ffn_mask': _L1_ffn_in['mask']}

def reference(x, ctx_4096, L0_xattn_Wq, L0_xattn_Wk, L0_xattn_Wv, L0_xattn_Wo, L0_attn_wq, L0_attn_wk, L0_attn_wv, L0_attn_wo, L0_ffn_weight, L0_ffn_bias, L0_ffn_lora_A, L0_ffn_lora_B, L0_ffn_lora_start_indices, L1_xattn_conv_w, L1_xattn_bn_gamma, L1_xattn_bn_beta, L1_attn_w_qkv, L1_attn_b_qkv, L1_attn_w_o, L1_attn_b_o, L1_ffn_W, L1_ffn_mask):
    import jax
    import jax.numpy as jnp

    def _L0_xattn_ref(latents, context, Wq, Wk, Wv, Wo):
        import jax, jax.numpy as jnp
        import numpy as np
        B, Q, D = (8, 64, 512)
        CTX = 512
        H, KV, HD = (16, 4, 96)
        G = H // KV
        b, q_len, _ = latents.shape
        hidden = jnp.concatenate([context, latents], axis=1)
        s_len = hidden.shape[1]
        q = (latents @ Wq.T).reshape(b, q_len, H, HD)
        k = (hidden @ Wk.T).reshape(b, s_len, KV, HD)
        v = (hidden @ Wv.T).reshape(b, s_len, KV, HD)
        q = q.transpose(0, 2, 1, 3).reshape(b, KV, G, q_len, HD)
        k = k.transpose(0, 2, 1, 3)
        v = v.transpose(0, 2, 1, 3)
        scale = 1.0 / jnp.sqrt(jnp.asarray(HD, q.dtype))
        scores = jnp.einsum('bkgqd,bksd->bkgqs', q, k) * scale
        attn = jax.nn.softmax(scores.astype(jnp.float32), axis=-1).astype(q.dtype)
        out = jnp.einsum('bkgqs,bksd->bkgqd', attn, v)
        out = out.reshape(b, H, q_len, HD).transpose(0, 2, 1, 3).reshape(b, q_len, H * HD)
        return out @ Wo.T

    def _L0_attn_ref(x, wq, wk, wv, wo):
        import jax, jax.numpy as jnp
        import numpy as np
        DIM = 512
        N_HEADS = 32
        N_KV_HEADS = 8
        HEAD_DIM = DIM // N_HEADS
        N_REP = N_HEADS // N_KV_HEADS
        THETA = 10000.0
        B, S = (4, 128)

        def _rope_cos_sin(seq_len):
            freqs = 1.0 / THETA ** (jnp.arange(0, HEAD_DIM, 2, dtype=jnp.float32) / HEAD_DIM)
            t = jnp.arange(seq_len, dtype=jnp.float32)
            ang = jnp.outer(t, freqs)
            return (jnp.cos(ang), jnp.sin(ang))

        def _apply_rope(x, cos, sin):
            xr = x[..., 0::2]
            xi = x[..., 1::2]
            c = cos[None, :, None, :]
            s = sin[None, :, None, :]
            out_r = xr * c - xi * s
            out_i = xr * s + xi * c
            return jnp.stack([out_r, out_i], axis=-1).reshape(x.shape)
        bsz, seq_len, _ = x.shape
        q = (x @ wq).reshape(bsz, seq_len, N_HEADS, HEAD_DIM)
        k = (x @ wk).reshape(bsz, seq_len, N_KV_HEADS, HEAD_DIM)
        v = (x @ wv).reshape(bsz, seq_len, N_KV_HEADS, HEAD_DIM)
        cos, sin = _rope_cos_sin(seq_len)
        q = _apply_rope(q, cos, sin)
        k = _apply_rope(k, cos, sin)
        k = jnp.repeat(k, N_REP, axis=2)
        v = jnp.repeat(v, N_REP, axis=2)
        scores = jnp.einsum('bqhd,bkhd->bhqk', q, k) / np.float32(np.sqrt(HEAD_DIM))
        mask = jnp.triu(jnp.full((seq_len, seq_len), -jnp.inf, dtype=scores.dtype), k=1)
        scores = scores + mask
        attn = jax.nn.softmax(scores.astype(jnp.float32), axis=-1).astype(q.dtype)
        out = jnp.einsum('bhqk,bkhd->bqhd', attn, v).reshape(bsz, seq_len, N_HEADS * HEAD_DIM)
        return out @ wo

    def _L0_ffn_ref(x, weight, bias, lora_A, lora_B, lora_start_indices):
        import jax, jax.numpy as jnp
        import numpy as np
        LORA_RANK = 16
        LORA_ALPHA = 16
        LORA_SCALE = LORA_ALPHA / LORA_RANK
        y = jnp.einsum('bsd,od->bso', x, weight) + bias
        B = x.shape[0]
        seg = jnp.searchsorted(lora_start_indices, jnp.arange(B), side='right') - 1
        adapter_idx = jnp.clip(seg - 1, 0, lora_A.shape[0] - 1)
        A = lora_A[adapter_idx]
        Bw = lora_B[adapter_idx]
        lo = jnp.einsum('bsr,bor->bso', jnp.einsum('bsd,brd->bsr', x, A), Bw) * LORA_SCALE
        use_lora = (seg > 0)[:, None, None]
        return y + jnp.where(use_lora, lo, jnp.zeros((), dtype=y.dtype))

    def _L1_xattn_ref(x, channel_map, conv_w, bn_gamma, bn_beta):
        import jax, jax.numpy as jnp
        import numpy as np
        import math
        EPS = 1e-05
        LAMBDA = 0.6

        def _crucial_k(C):
            f = math.floor(LAMBDA * C)
            return f + f % 2

        def _conv1d(y, w):
            return jax.lax.conv_general_dilated(y, w, window_strides=(1,), padding=((3, 3),), dimension_numbers=('NCH', 'OIH', 'NCH'))

        def _norm_active(z, gamma, beta):
            mu = jnp.mean(z, axis=(0, 2), keepdims=True)
            var = jnp.mean((z - mu) ** 2, axis=(0, 2), keepdims=True)
            zn = (z - mu) * jax.lax.rsqrt(var + EPS)
            zn = zn * gamma.reshape(1, -1, 1) + beta.reshape(1, -1, 1)
            return jax.nn.sigmoid(jax.nn.relu(zn))
        B, C, L = x.shape
        k = _crucial_k(C)
        cm = jnp.moveaxis(channel_map, 1, 2)
        _, topk_idx = jax.lax.top_k(cm, k)
        b_idx = jnp.arange(B)[:, None, None]
        l_idx = jnp.arange(L)[None, :, None]
        mask = jnp.zeros((B, L, C), x.dtype).at[b_idx, l_idx, topk_idx].set(1.0)
        crucial_channels = jnp.moveaxis(mask, 2, 1)
        subcrucial_channels = 1.0 - crucial_channels
        crucial_features = crucial_channels * x
        subcrucial_features = subcrucial_channels * x
        c_max = jnp.max(crucial_features, axis=1, keepdims=True)
        c_avg = jnp.mean(crucial_features, axis=1, keepdims=True) * (C / k)
        s_max = jnp.max(subcrucial_features, axis=1, keepdims=True)
        s_avg = jnp.mean(subcrucial_features, axis=1, keepdims=True) * (C / (C - k))
        crucial_x = jnp.concatenate([c_max, c_avg], axis=1)
        subcrucial_x = jnp.concatenate([s_max, s_avg], axis=1)
        A_S1 = _norm_active(_conv1d(crucial_x, conv_w), bn_gamma, bn_beta)
        A_S2 = _norm_active(_conv1d(subcrucial_x, conv_w), bn_gamma, bn_beta)
        return crucial_features * A_S1 + subcrucial_features * A_S2

    def _L1_attn_ref(x, w_qkv, b_qkv, w_o, b_o):
        import jax, jax.numpy as jnp
        import numpy as np
        B, S, HIDDEN = (2, 256, 512)
        TP = 2
        PART = HIDDEN // TP
        NUM_HEADS = 16 // TP
        HEAD_DIM = PART // NUM_HEADS
        MASKED_BIAS = -10000.0
        b, s, _ = x.shape
        qkv = x @ w_qkv.T + b_qkv
        q, k, v = jnp.split(qkv, 3, axis=-1)

        def to_heads(a):
            return a.reshape(b, s, NUM_HEADS, HEAD_DIM).transpose(0, 2, 1, 3)
        q, k, v = (to_heads(q), to_heads(k), to_heads(v))
        scores = jnp.einsum('bhfc,bhtc->bhft', k, q)
        causal = jnp.triu(jnp.ones((s, s), dtype=bool))
        scores = jnp.where(causal[None, None], scores, MASKED_BIAS)
        attn = jax.nn.softmax(scores, axis=-2)
        vals = jnp.einsum('bhft,bhfc->bhtc', attn, v)
        vals = vals.transpose(0, 2, 1, 3).reshape(b, s, PART)
        out = vals @ w_o.T + b_o
        return out

    def _L1_ffn_ref(x, W, mask):
        import jax, jax.numpy as jnp
        import numpy as np
        HIDDEN = 512
        SPARSITY_RATIO = 0.1
        BLOCK_SIZE = max(1, int(HIDDEN * SPARSITY_RATIO * 2))

        def _block_diag_mask(h: int, block_size: int) -> jnp.ndarray:
            idx = jnp.arange(h) // block_size
            return idx[:, None] == idx[None, :]
        sparse_W = W * mask.astype(W.dtype)
        return jnp.einsum('bsh,oh->bso', x, sparse_W)
    x = x + _L0_xattn_ref(_layernorm(x, axis=-1), ctx_4096, L0_xattn_Wq, L0_xattn_Wk, L0_xattn_Wv, L0_xattn_Wo)
    x = x + _L0_attn_ref(_layernorm(x, axis=-1), L0_attn_wq, L0_attn_wk, L0_attn_wv, L0_attn_wo)
    x = x + _L0_ffn_ref(_layernorm(x, axis=-1), L0_ffn_weight, L0_ffn_bias, L0_ffn_lora_A, L0_ffn_lora_B, L0_ffn_lora_start_indices)
    x = x + _L1_xattn_ref(_layernorm(x, axis=-1), ctx_4096, L1_xattn_conv_w, L1_xattn_bn_gamma, L1_xattn_bn_beta)
    x = x + _L1_attn_ref(_layernorm(x, axis=-1), L1_attn_w_qkv, L1_attn_b_qkv, L1_attn_w_o, L1_attn_b_o)
    x = x + _L1_ffn_ref(_layernorm(x, axis=-1), L1_ffn_W, L1_ffn_mask)
    return x

_drawn_inputs = setup_inputs


def setup_inputs(seed=0):
    import zlib

    import numpy as np

    out = dict(_drawn_inputs(seed))
    spreads = {}
    factors = {'L0_xattn_Wq': 4.729,
     'L0_xattn_Wk': 4.729,
     'L0_ffn_bias': 8.0,
     'L1_attn_b_qkv': 8.0,
     'L1_attn_b_o': 6.501}
    for name, (base, spread) in spreads.items():
        noise = np.random.default_rng([zlib.crc32(name.encode()), seed]).standard_normal(out[name].shape)
        drawn = base * np.exp(spread * noise) if base else spread * noise
        out[name] = jnp.asarray(drawn.astype(out[name].dtype))
    for name, factor in factors.items():
        out[name] = (out[name] * factor).astype(out[name].dtype)
    return out
```

```python
from contextlib import ExitStack

import numpy as np

import concourse.bass as bass
from concourse import mybir

F32 = mybir.dt.float32
I32 = mybir.dt.int32
U8 = mybir.dt.uint8
ALU = mybir.AluOpType
ACT = mybir.ActivationFunctionType
AX = mybir.AxisListType

P = 128
B, L, D = 64, 32, 512
CTX = 257
DC = D // P
TB = P // L
NT = B // TB
EPS = 1e-5

KVH, G, HD = 4, 4, 96
KW = KVH * HD
NKT = KW // P
S = CTX + L
TAIL = L + 1
XSCALE = 1.0 / float(np.sqrt(np.float32(HD)))
TOPK = 20
GONE = -3.0e38

K_ROWS = [(0, 0, 96), (1, 0, 32), (1, 32, 96), (2, 0, 64), (3, 0, 96), (2, 64, 96)]
PAIRS = [(0, 0, 0, 96), (1, 0, 96, 128), (1, 1, 0, 64), (2, 1, 64, 128), (2, 2, 96, 128), (3, 2, 0, 96)]
PAIRS_OF_HEAD = [[n for n, x in enumerate(PAIRS) if x[0] == g] for g in range(KVH)]


LANES = 4
AKVH, AG, AD = 8, 4, 16
AQ, AKV = AKVH * AG * AD, AKVH * AD
QKH = AKVH * (AG + 1)
ASCALE = 0.25
NLR, BIAS_ROW = 48, 64
L0_LOADS = 14
TAPS = 7
EH, EW = 8, 256


def wait(eng, sem, value):
    if not isinstance(value, int) or value > 0:
        eng.wait_ge(sem, value)


def build_program(nc, a, last_phase=9):
    ctx = ExitStack()
    with ctx:
        def sb(name, shape, dt=F32):
            return ctx.enter_context(nc.sbuf_tensor(name, shape, dt))

        def sem(name):
            return ctx.enter_context(nc.semaphore(name))

        X = sb("X", [P, NT * D])
        mask = sb("mask", [P, DC, B * L], U8)
        ident = sb("ident", [P, P])
        neghalf = sb("neghalf", [P, 1])

        def x_tile(t):
            return X[:, bass.ts(t, D)]

        phase_a(nc, a, X, mask, ident, neghalf, x_tile)
        if last_phase == 1:
            dump(nc, a, X)
            return
        phase_rest(nc, a, X, mask, ident, neghalf, x_tile, last_phase)


def dump(nc, a, X):
    with nc.semaphore("dump_out") as out_done, nc.Block() as block:
        @block.sync
        def _(sp):
            sp.dma_start(a["y"].rearrange("t p d -> p t d"), X[:].rearrange("p (t d) -> p t d", d=D)).then_inc(out_done, 16)
            sp.wait_ge(out_done, 16)


def phase_a(nc, a, X, mask, ident, neghalf, x_tile):
    ctx = ExitStack()
    with ctx:
        def sb(name, shape, dt=F32):
            return ctx.enter_context(nc.sbuf_tensor(name, shape, dt))

        def psum(name, shape):
            return ctx.enter_context(nc.psum_tensor(name, shape, F32))

        def sem(name):
            return ctx.enter_context(nc.semaphore(name))

        WqT = sb("WqT", [P, DC, NKT * G * P])
        WkT = sb("WkT", [P, DC, KW])
        WvT = sb("WvT", [P, DC, KW])
        WoT = sb("WoT", [P, NKT * G, D])
        clast = sb("clast", [P, DC, B])
        hid = sb("hid", [P, TB, DC, S])
        xn = sb("xn", [P, D])
        xnT = sb("xnT", [P, DC, P])
        QT = sb("QT", [P, len(PAIRS), TB, G * L])
        KT = sb("KT", [P, 2, NKT, S])
        V = sb("V", [P, 2, 2, KW])
        Vlat = sb("Vlat", [P, KW])
        Vtail = sb("Vtail", [TAIL, TB, KW])
        probs = sb("probs", [P, KVH, S])
        probsT = sb("probsT", [P, 2, 3, P])
        O = sb("O", [P, KW])
        OT = sb("OT", [P, NKT, G, TB, L])
        work = sb("work", [P, DC, CTX])
        top = [sb(f"top{k}", [P, DC, 8]) for k in range(3)]
        top_last = sb("top_last", [P, DC, 8])
        gate = sb("gate", [P, 1])
        rmax = sb("rmax", [P, KVH])
        nmax = sb("nmax", [P, KVH])
        rsum = sb("rsum", [P, 2, KVH])
        rinv = sb("rinv", [P, KVH])
        stats = sb("stats", [P, 6])
        mv = sb("mv", [P, 2])
        veps = sb("veps", [P, 1])
        rstd = sb("rstd", [P, 1])
        vlast_dram = nc.dram_tensor("vlast_dram", [B, KW], F32, kind="Internal").ap()

        psKV = psum("psKV", [P, 2, 512])
        psS = psum("psS", [P, 2, 512])
        psPT = psum("psPT", [P, 2, 512])
        psO = psum("psO", [P, 512])
        psM = psum("psM", [P, 512])

        const_in = sem("const_in")
        x0_in = sem("x0_in")
        x_in = sem("x_in")
        wv_in = sem("wv_in")
        wq_in = sem("wq_in")
        wk_in = sem("wk_in")
        wo_in = sem("wo_in")
        ctx_in = [sem(f"ctx_in{j}") for j in range(TB)]
        zero_done = sem("zero_done")
        vlast_filled = sem("vlast_filled")
        vlast_evac = sem("vlast_evac")
        vlast_out = sem("vlast_out")
        vtail_in = sem("vtail_in")
        kv_filled = sem("kv_filled")
        kv_evac = sem("kv_evac")
        s_filled = sem("s_filled")
        rmax_done = sem("rmax_done")
        nmax_ready = sem("nmax_ready")
        exp_done = sem("exp_done")
        pt_filled = sem("pt_filled")
        pt_evac = sem("pt_evac")
        av_done = sem("av_done")
        recip_done = sem("recip_done")
        o_evac = sem("o_evac")
        m_filled = sem("m_filled")
        m_evac = sem("m_evac")
        topk_step = sem("topk_step")
        stats_done = sem("stats_done")
        veps_ready = sem("veps_ready")
        rstd_ready = sem("rstd_ready")
        xn_ready = sem("xn_ready")

        def kv(t, n):
            if isinstance(t, int) and t == 0 and n < 5:
                return 1 + n
            if isinstance(t, int) and t == -1 and n > 20:
                return 6 + n - 21
            return 4 + 24 * t + n

        def kv_bank(t, n):
            return (kv(t, n) if isinstance(t, int) else n) % 2

        def m_ot(t, j):
            return 6 * t + 1 + j if j < TB - 1 else 6 * (t + 1) - 1 - (1 if isinstance(t, int) and t == NT - 1 else 0)

        def m_proj(t):
            return m_ot(t, TB - 1) + 1

        def m_xt(t):
            return 6 * (t - 1) + 4 if not (isinstance(t, int) and t == 0) else 0

        def over_tiles(eng, body):
            body(0, True, False)
            with eng.Fori(1, NT - 1) as t:
                body(t, False, False)
            body(NT - 1, False, True)

        block = ctx.enter_context(nc.Block())

        @block.sync
        def _(sp):
            sp.dma_start(ident[:], a["ident"]).then_inc(const_in, 16)
            x_v = X[:].rearrange("p (t d) -> p t d", d=D)
            sp.dma_start(x_v[:, 0:1], a["x"][:, 0:1]).then_inc(x0_in, 16)
            sp.dma_start(clast[:], a["ctx_last"]).then_inc(const_in, 16)
            sp.dma_start(WvT[:], a["WvT"]).then_inc(wv_in, 16)
            sp.dma_start(WkT[:], a["WkT"]).then_inc(wk_in, 16)
            sp.dma_start(hid[:, 0, :, 0:CTX], a["ctxT"][0]).then_inc(ctx_in[0], 16)
            for c in range(DC):
                sp.dma_start(WqT[:, c], a["WqT"][:, c]).then_inc(wq_in, 16)
            for j in range(1, TB):
                sp.dma_start(hid[:, j, :, 0:CTX], a["ctxT"][j]).then_inc(ctx_in[j], 16)
            sp.dma_start(x_v[:, 1:NT], a["x"][:, 1:NT]).then_inc(x_in, 16)
            sp.dma_start(WoT[:], a["WoT"]).then_inc(wo_in, 16)
            sp.wait_ge(vlast_evac, 1)
            sp.dma_start(vlast_dram, O[0:B, :]).then_inc(vlast_out, 16)
            sp.wait_ge(vlast_out, 16)

            def load_tail(t):
                wait(sp, av_done, 16 * t)
                sp.dma_start(Vtail[0:1, :, :].rearrange("a j n -> a (j n)"),
                             vlast_dram[bass.ts(t, TB), :].rearrange("(a j) n -> a (j n)", a=1)).then_inc(vtail_in, 16)
                wait(sp, kv_evac, kv(t - 1, 20) + 1)
                for j in range(TB):
                    sp.dma_start(Vtail[1:TAIL, j, :], Vlat[L * j:L * j + L, :]).then_inc(vtail_in, 16)

            load_tail(0)

            def body(t, first, last):
                if last:
                    return
                for j in range(TB):
                    sp.wait_ge(kv_filled, kv(t, 5 * j + 4) + 1)
                    sp.wait_ge(topk_step, 8 * (TB * t + j) + 2)
                    sp.dma_start(hid[:, j, :, 0:CTX], a["ctxT"][TB * (t + 1) + j]).then_inc(ctx_in[j], 16)
                load_tail(t + 1)

            over_tiles(sp, body)

        @block.gpsimd
        def _(pool):
            pool.memset(neghalf[:], -0.5).then_inc(zero_done, 1)
            pool.memset(QT[:], 0.0).then_inc(zero_done, 1)
            pool.memset(top_last[:], GONE).then_inc(zero_done, 1)
            pool.wait_ge(zero_done, 3)

            def rstd_of(t):
                wait(pool, xn_ready, t)
                pool.wait_ge(veps_ready, t + 1)
                pool.tensor_tensor(rstd[:], veps[:], neghalf[:], ALU.pow).then_inc(rstd_ready, 1)

            rstd_of(0)
            with pool.Fori(1, NT) as t:
                rstd_of(t)

        @block.tensor
        def _(pe):
            def next_bank(t, n):
                wait(pe, kv_evac, kv(t, n) - 1)
                return psKV[:, kv_bank(t, n), :]

            def xt(t):
                pe.wait_ge(xn_ready, t + 1)
                wait(pe, m_evac, m_xt(t))
                for c in range(DC):
                    mm = pe.transpose(psM[:, P * c:P * c + P], xn[:, P * c:P * c + P], ident[:])
                mm.then_inc(m_filled, 1)

            def v_latents(t):
                out = next_bank(t - 1, 20)
                pe.wait_ge(m_evac, m_xt(t) + 1)
                for c in range(DC):
                    mm = pe.matmul(out[:, 0:KW], xnT[:, c, :], WvT[:, c, :], start=(c == 0), stop=(c == DC - 1))
                mm.then_inc(kv_filled, 1)

            def q(t, k):
                out = next_bank(t - 1, 21 + k)
                for r in range(G):
                    for c in range(DC):
                        w = P * (G * k + r)
                        mm = pe.matmul(out[:, P * r:P * r + P], WqT[:, c, w:w + P], xnT[:, c, :],
                                       start=(c == 0), stop=(c == DC - 1))
                mm.then_inc(kv_filled, 1)

            def k_part(t, j, k):
                out = next_bank(t, 5 * j + k)
                if k == 0:
                    pe.wait_ge(ctx_in[j], 16 * (t + 1))
                    pe.wait_ge(m_evac, m_xt(t) + 1)
                for c in range(DC):
                    mm = pe.matmul(out[:, 0:S], WkT[:, c, P * k:P * k + P], hid[:, j, c, :],
                                   start=(c == 0), stop=(c == DC - 1))
                mm.then_inc(kv_filled, 1)

            def v_part(t, j, s):
                out = next_bank(t, 5 * j + 3 + s)
                for c in range(DC):
                    mm = pe.matmul(out[:, 0:KW], hid[:, j, c, P * s:P * s + P], WvT[:, c, :],
                                   start=(c == 0), stop=(c == DC - 1))
                mm.then_inc(kv_filled, 1)

            def scores(t, j, h):
                b = TB * t + j
                wait(pe, exp_done, 4 * b + 2 * h)
                if h == 0:
                    pe.wait_ge(kv_evac, kv(t, 5 * j + 2) + 1)
                for g in (2 * h, 2 * h + 1):
                    ps = PAIRS_OF_HEAD[g]
                    for n, p in enumerate(ps):
                        mm = pe.matmul(psS[:, g % 2, 0:S], QT[:, p, j, :], KT[:, j % 2, PAIRS[p][1], :],
                                       start=(n == 0), stop=(n == len(ps) - 1))
                mm.then_inc(s_filled, 1)

            def turn_probs(t, j, g):
                at = 4 * (TB * t + j) + g
                pe.wait_ge(exp_done, at + 1)
                wait(pe, pt_evac, at - 1)
                for k, (lo, hi) in enumerate(((0, P), (P, 2 * P), (2 * P, S))):
                    mm = pe.transpose(psPT[0:hi - lo, g % 2, P * k:P * k + P], probs[:, g, lo:hi], ident[:])
                mm.then_inc(pt_filled, 1)

            def values(t, j, g):
                b = TB * t + j
                pe.wait_ge(pt_evac, 4 * b + g + 1)
                if g == 0:
                    pe.wait_ge(kv_evac, kv(t, 5 * j + 4) + 1)
                    pe.wait_ge(vtail_in, 80 * (t + 1))
                    wait(pe, o_evac, b)
                out = psO[:, HD * g:HD * g + HD]
                cols = slice(HD * g, HD * g + HD)
                pe.matmul(out, probsT[:, g % 2, 0, :], V[:, j % 2, 0, cols], start=True, stop=False)
                pe.matmul(out, probsT[:, g % 2, 1, :], V[:, j % 2, 1, cols], start=False, stop=False)
                pe.matmul(out, probsT[0:TAIL, g % 2, 2, :], Vtail[:, j, cols],
                          start=False, stop=True).then_inc(av_done, 1)

            def turn_out(t, j):
                pe.wait_ge(m_evac, m_ot(t, j))
                pe.wait_ge(o_evac, TB * t + j + 1)
                for k in range(NKT):
                    mm = pe.transpose(psM[:, P * k:P * k + P], O[:, P * k:P * k + P], ident[:])
                mm.then_inc(m_filled, 1)

            def project(t):
                pe.wait_ge(m_evac, m_proj(t))
                for n in range(NKT * G):
                    mm = pe.matmul(psM[:], OT[:, n // G, n % G].rearrange("p j q -> p (j q)"), WoT[:, n, :],
                                   start=(n == 0), stop=(n == NKT * G - 1))
                mm.then_inc(m_filled, 1)

            pe.wait_ge(const_in, 32)
            pe.wait_ge(wv_in, 16)
            for c in range(DC):
                mm = pe.matmul(psS[0:B, 0, 0:KW], clast[:, c, :], WvT[:, c, :], start=(c == 0), stop=(c == DC - 1))
            mm.then_inc(vlast_filled, 1)
            xt(0)
            v_latents(0)
            pe.wait_ge(wk_in, 16)
            pe.wait_ge(vlast_evac, 1)

            def body(t, first, last):
                k_part(t, 0, 0)
                k_part(t, 0, 1)
                if not first:
                    turn_out(t - 1, TB - 1)
                k_part(t, 0, 2)
                v_part(t, 0, 0)
                v_part(t, 0, 1)
                if first:
                    pe.wait_ge(wq_in, 64)
                    for k in range(NKT):
                        q(0, k)
                    pe.wait_ge(kv_evac, kv(-1, 23) + 1)
                else:
                    project(t - 1)
                for j in range(TB):
                    scores(t, j, 0)
                    if j < TB - 1:
                        k_part(t, j + 1, 0)
                        if j:
                            turn_out(t, j - 1)
                        k_part(t, j + 1, 1)
                    else:
                        v_part(t, j, 1)
                        turn_out(t, j - 1)
                    turn_probs(t, j, 0)
                    turn_probs(t, j, 1)
                    if j == TB - 1 and not last:
                        xt(t + 1)
                    scores(t, j, 1)
                    values(t, j, 0)
                    if j < TB - 1:
                        k_part(t, j + 1, 2)
                        values(t, j, 1)
                        if j < TB - 2:
                            v_part(t, j + 1, 0)
                            turn_probs(t, j, 2)
                            turn_probs(t, j, 3)
                            v_part(t, j + 1, 1)
                        else:
                            turn_probs(t, j, 2)
                            turn_probs(t, j, 3)
                            v_part(t, j + 1, 0)
                    else:
                        if not last:
                            v_latents(t + 1)
                        values(t, j, 1)
                        if not last:
                            q(t + 1, 0)
                        turn_probs(t, j, 2)
                        turn_probs(t, j, 3)
                        if not last:
                            q(t + 1, 1)
                            q(t + 1, 2)
                    values(t, j, 2)
                    values(t, j, 3)
                if first:
                    pe.wait_ge(wo_in, 16)

            over_tiles(pe, body)
            turn_out(NT - 1, TB - 1)
            project(NT - 1)

        @block.scalar
        def _(act):
            def evac_k(t, j, k):
                act.wait_ge(kv_filled, kv(t, 5 * j + k) + 1)
                if k == 0:
                    wait(act, s_filled, 2 * (TB * t + j) - 2)
                act.activation(KT[:, j % 2, k, :], psKV[:, kv_bank(t, 5 * j + k), 0:S], ACT.Copy).then_inc(kv_evac, 1)

            def evac_v(t, j, s):
                act.wait_ge(kv_filled, kv(t, 5 * j + 3 + s) + 1)
                if s == 0:
                    wait(act, av_done, 4 * (TB * t + j) - 4)
                act.activation(V[:, j % 2, s, :], psKV[:, kv_bank(t, 5 * j + 3 + s), 0:KW], ACT.Copy).then_inc(kv_evac, 1)

            def evac_v_latents(t):
                wait(act, vtail_in, 80 * t)
                act.wait_ge(kv_filled, kv(t - 1, 20) + 1)
                act.activation(Vlat[:], psKV[:, kv_bank(t - 1, 20), 0:KW], ACT.Copy).then_inc(kv_evac, 1)

            def evac_q(t, k):
                wait(act, s_filled, 2 * TB * t)
                act.wait_ge(kv_filled, kv(t - 1, 21 + k) + 1)
                src = psKV[:, kv_bank(t - 1, 21 + k), :].rearrange("p (r j q) -> p r j q", r=G, j=TB)
                parts = [n for n, x in enumerate(PAIRS) if x[1] == k]
                for n in parts:
                    lo, hi = PAIRS[n][2:]
                    ins = act.activation(QT[lo:hi, n].rearrange("p j (r q) -> p r j q", r=G), src[lo:hi], ACT.Copy)
                ins.then_inc(kv_evac, 1)

            def exps(t, j, h):
                b = TB * t + j
                act.wait_ge(nmax_ready, 2 * b + h + 1)
                wait(act, pt_filled, 4 * b + 2 * h - 2)
                if h == 0:
                    wait(act, recip_done, b - 1)
                for g in (2 * h, 2 * h + 1):
                    act.activation(probs[:, g, :], psS[:, g % 2, 0:S], ACT.Exp, bias=nmax[:, g:g + 1],
                                   scale=XSCALE, accum_out=rsum[:, j % 2, g:g + 1]).then_inc(exp_done, 1)

            def evac_probs(t, j, g):
                at = 4 * (TB * t + j) + g
                act.wait_ge(pt_filled, at + 1)
                wait(act, av_done, at - 1)
                act.activation(probsT[:, g % 2, 0:2, :].rearrange("p a q -> p (a q)"), psPT[:, g % 2, 0:2 * P], ACT.Copy)
                act.activation(probsT[0:TAIL, g % 2, 2, :], psPT[0:TAIL, g % 2, 2 * P:3 * P],
                               ACT.Copy).then_inc(pt_evac, 1)

            act.wait_ge(vlast_filled, 1)
            act.activation(O[0:B, :], psS[0:B, 0, 0:KW], ACT.Copy).then_inc(vlast_evac, 1)
            evac_v_latents(0)

            def body(t, first, last):
                for k in range(NKT):
                    evac_k(t, 0, k)
                evac_v(t, 0, 0)
                evac_v(t, 0, 1)
                if first:
                    act.wait_ge(zero_done, 3)
                    for k in range(NKT):
                        evac_q(0, k)
                for j in range(TB):
                    exps(t, j, 0)
                    if j < TB - 1:
                        evac_k(t, j + 1, 0)
                        evac_k(t, j + 1, 1)
                    else:
                        evac_v(t, j, 1)
                    evac_probs(t, j, 0)
                    evac_probs(t, j, 1)
                    exps(t, j, 1)
                    if j < TB - 2:
                        evac_k(t, j + 1, 2)
                        evac_v(t, j + 1, 0)
                        evac_probs(t, j, 2)
                        evac_probs(t, j, 3)
                        evac_v(t, j + 1, 1)
                    elif j == TB - 2:
                        evac_k(t, j + 1, 2)
                        evac_probs(t, j, 2)
                        evac_probs(t, j, 3)
                        evac_v(t, j + 1, 0)
                    else:
                        if not last:
                            evac_v_latents(t + 1)
                            evac_q(t + 1, 0)
                        evac_probs(t, j, 2)
                        evac_probs(t, j, 3)
                        if not last:
                            evac_q(t + 1, 1)
                            evac_q(t + 1, 2)

            over_tiles(act, body)

        @block.vector
        def _(dve):
            def norm_stats(t):
                wait(dve, xn_ready, t)
                dve.bn_stats(stats[:], x_tile(t)).then_inc(stats_done, 1)
                dve.wait_ge(stats_done, 2 * t + 1)
                wait(dve, rstd_ready, t)
                dve.memset(gate[:], 0.0)
                dve.bn_aggr(mv[:], stats[:]).then_inc(stats_done, 1)
                dve.wait_ge(stats_done, 2 * t + 2)
                dve.tensor_scalar(veps[:], mv[:, 1:2], EPS, None, ALU.add).then_inc(veps_ready, 1)

            def norm(t):
                dve.wait_ge(rstd_ready, t + 1)
                wait(dve, m_filled, m_xt(t - 1) + 1 if not (isinstance(t, int) and t == 0) else 0)
                dve.tensor_scalar(xn[:], x_tile(t), mv[:, 0:1], rstd[:, 0:1], ALU.subtract, ALU.mult)\
                   .then_inc(xn_ready, 1)

            def evac_xt(t):
                wait(dve, kv_filled, kv(t - 1, 20))
                dve.wait_ge(m_filled, m_xt(t) + 1)
                dve.tensor_copy(xnT[:].rearrange("p c q -> p (c q)"), psM[:])
                dve.tensor_copy(hid[:, :, :, CTX:S], psM[:].rearrange("p (c j q) -> p j c q", c=DC, j=TB))\
                   .then_inc(m_evac, 1)

            def row_max(t, j, h):
                b = TB * t + j
                dve.wait_ge(s_filled, 2 * b + h + 1)
                wait(dve, nmax_ready, 2 * b + h)
                dve.tensor_reduce(rmax[:, 2 * h:2 * h + 2], psS[:, :, 0:S], AX.X, ALU.max).then_inc(rmax_done, 1)
                dve.wait_ge(rmax_done, 2 * b + h + 1)
                wait(dve, exp_done, 4 * b + 2 * h - 2)
                dve.tensor_scalar(nmax[:, 2 * h:2 * h + 2], rmax[:, 2 * h:2 * h + 2], -XSCALE, None, ALU.mult)\
                   .then_inc(nmax_ready, 1)

            def evac_out(t, j):
                b = TB * t + j
                dve.wait_ge(exp_done, 4 * b + 4)
                wait(dve, o_evac, b)
                dve.reciprocal(rinv[:], rsum[:, j % 2, :]).then_inc(recip_done, 1)
                dve.wait_ge(recip_done, b + 1)
                dve.wait_ge(av_done, 4 * b + 4)
                wait(dve, m_filled, m_ot(t, j) if j else m_ot(t, 0) - 1)
                dve.tensor_tensor(O[:].rearrange("p (g d) -> p g d", g=KVH),
                                  psO[:, 0:KW].rearrange("p (g d) -> p g d", g=KVH),
                                  rinv[:].unsqueeze(2).to_broadcast([P, KVH, HD]), ALU.mult).then_inc(o_evac, 1)

            def evac_ot(t, j):
                dve.wait_ge(m_filled, m_ot(t, j) + 1)
                dve.tensor_copy(OT[:, :, :, j, :], psM[:, 0:KW].rearrange("p (k r q) -> p k r q", k=NKT, r=G))\
                   .then_inc(m_evac, 1)

            def add_projected(t):
                dve.wait_ge(m_filled, m_proj(t) + 1)
                dve.tensor_tensor(x_tile(t), x_tile(t), psM[:], ALU.add).then_inc(m_evac, 1)

            def topk(t, j, step):
                b = TB * t + j
                if step in (1, 2, 3, 4, 5, 7):
                    wait(dve, topk_step, 8 * b + step - 1)
                    if step == 1:
                        dve.wait_ge(ctx_in[j], 16 * (t + 1))
                    dve.memset(gate[:], 0.0)
                src = hid[:, j, :, 0:CTX]
                if step in (1, 3, 5):
                    for c in range(DC):
                        ins = dve.max(top[step // 2][:, c, :], src[:, c, :] if step == 1 else work[:, c, :])
                elif step in (2, 4, 7):
                    picked = {2: top[0], 4: top[1], 7: top_last}[step]
                    for c in range(DC):
                        ins = dve.match_replace(work[:, c, :], picked[:, c, :],
                                                src[:, c, :] if step == 2 else work[:, c, :], GONE)
                elif step == 6:
                    dve.wait_ge(topk_step, 8 * b + 5)
                    ins = dve.tensor_copy(top_last[:, :, 0:4], top[2][:, :, 0:4])
                else:
                    dve.wait_ge(topk_step, 8 * b + 7)
                    ins = dve.tensor_scalar(mask[:, :, bass.ts(b, L)], work[:, :, 0:L], GONE, None, ALU.is_le)
                ins.then_inc(topk_step, 1)

            dve.wait_ge(x0_in, 16)
            norm_stats(0)
            norm(0)
            evac_xt(0)
            dve.wait_ge(zero_done, 3)
            dve.wait_ge(x_in, 16)
            dve.wait_ge(vlast_out, 16)

            def body(t, first, last):
                if not first:
                    evac_out(t - 1, TB - 1)
                    evac_ot(t - 1, TB - 1)
                    add_projected(t - 1)
                for j in range(TB):
                    if j:
                        evac_out(t, j - 1)
                    row_max(t, j, 0)
                    topk(t, j, 1)
                    if j:
                        evac_ot(t, j - 1)
                    if j == TB - 1 and not last:
                        evac_xt(t + 1)
                    topk(t, j, 2)
                    if j == 1 and not last:
                        norm_stats(t + 1)
                    if j == 2 and not last:
                        norm(t + 1)
                    row_max(t, j, 1)
                    for step in range(3, 9):
                        topk(t, j, step)

            over_tiles(dve, body)
            evac_out(NT - 1, TB - 1)
            evac_ot(NT - 1, TB - 1)
            add_projected(NT - 1)


def phase_rest(nc, a, X, mask, ident, neghalf, x_tile, last_phase):
    ctx = ExitStack()
    with ctx:
        def sb(name, shape, dt=F32):
            return ctx.enter_context(nc.sbuf_tensor(name, shape, dt))

        posT = sb("posT", [P, DC, NT * P])
        Y = sb("Y", [P, DC, 2, 2, B])
        lanes = sb("lanes", [P, LANES, 2, 1024])
        xn = sb("lane_xn", [P, LANES, D])
        xnT = sb("lane_xnT", [P, LANES, DC, P])
        small = {k: sb(f"lane_{k}", [P, LANES, n]) for k, n in
                 (("stats", 6), ("mv", 2), ("veps", 1), ("rstd", 1), ("rmax", 32), ("rinv", 32), ("rsum", 8))}
        jmask = sb("jmask", [P, TB])
        ones = sb("ones", [P, P])
        bufs = (posT, Y, lanes, xn, xnT, small, jmask, ones)
        blend = sb("blend", [P, DC, 2, B])

        with nc.psum_tensor("psLane", [P, LANES, 1024], F32) as ps:
            layer0(nc, a, X, mask, ident, neghalf, x_tile, ps, bufs)
            if last_phase <= 3:
                dump(nc, a, X)
                return
            mix_gates(nc, a, neghalf, ps, Y, ones, blend)
            layer1(nc, a, X, mask, ident, neghalf, x_tile, ps, bufs, blend)


def norm_sems(sem, name):
    return {k: sem(f"{name}_{k}") for k in ("stats", "aggr", "veps", "rstd", "xn", "xt", "xnT")}


def norm_stats(dve, n, t, u, x, small, gate, before):
    before()
    dve.memset(gate[:], 0.0)
    dve.bn_stats(small["stats"][:, u], x).then_inc(n["stats"], 1)
    dve.wait_ge(n["stats"], t + 1)
    dve.memset(gate[:], 0.0)
    dve.bn_aggr(small["mv"][:, u], small["stats"][:, u]).then_inc(n["aggr"], 1)
    dve.wait_ge(n["aggr"], t + 1)
    dve.tensor_scalar(small["veps"][:, u], small["mv"][:, u, 1:2], EPS, None, ALU.add).then_inc(n["veps"], 1)


def norm_rstd(pool, n, t, u, small, neghalf):
    pool.wait_ge(n["veps"], t + 1)
    pool.tensor_tensor(small["rstd"][:, u], small["veps"][:, u], neghalf[:], ALU.pow).then_inc(n["rstd"], 1)


def norm_rows(dve, n, t, u, x, small, xn):
    dve.wait_ge(n["rstd"], t + 1)
    dve.tensor_scalar(xn[:, u], x, small["mv"][:, u, 0:1], small["rstd"][:, u, 0:1],
                      ALU.subtract, ALU.mult).then_inc(n["xn"], 1)


def norm_turn(pe, n, t, u, xn, out, ident):
    pe.wait_ge(n["xn"], t + 1)
    for c in range(DC):
        mm = pe.transpose(out[:, P * c:P * c + P], xn[:, u, P * c:P * c + P], ident[:])
    mm.then_inc(n["xt"], 1)


SLOTS0 = {
    "stats1": 0.159, "rstd1": 0.252, "rows1": 0.265, "turn1": 0.265, "xnT1": 0.312, "qkv": 0.363, "rope": 0.787,
    "spread_v": 0.796, "rope_sum": 0.994, "turn_qk": 0.994, "evac_q": 1.153, "spread_k": 0.994, "scores": 1.153,
    "mask": 1.381, "shift": 1.393, "exps": 1.469, "turn_probs": 1.554, "evac_pt": 1.559, "values": 1.738,
    "normalise": 1.884, "turn_out": 1.903, "evac_ot": 1.936, "project": 2.028, "add_proj": 2.251,
    "stats2": 2.293, "rstd2": 2.293, "rows2": 2.514, "turn2": 2.530, "xnT2": 2.558, "lora_down": 2.569,
    "lora_mask": 2.737, "ffn": 2.753, "lora_up": 3.319, "add_ffn": 3.511, "stats3": 3.541, "rstd3": 3.541,
    "rows3": 3.560, "turn3": 3.560, "pos": 3.560, "crucial": 3.588, "rest": 3.702, "reduce": 3.889,}
SLOTS1 = {
    "gate": 0.123, "add_rest": 0.123, "mix": 0.266, "turn_mix": 0.343, "add_mix": 0.355, "stats1": 0.547,
    "rstd1": 0.547, "rows1": 0.858, "bias": 1.004, "turn1": 0.866, "xnT1": 1.018, "qkv": 1.080,
    "evac_qk": 1.148, "evac_v": 2.153, "spread_k": 1.482, "scores": 1.738, "mask": 1.910, "shift": 1.938,
    "exps": 2.034, "spread_p": 2.168, "turn_probs": 2.259, "evac_pt": 2.289, "values": 2.483,
    "normalise": 2.738, "turn_out": 2.747, "evac_ot": 2.913, "project": 2.913, "add_proj": 3.125,
    "stats2": 3.125, "rstd2": 3.137, "rows2": 3.137, "turn2": 3.137, "xnT2": 3.137, "ffn": 3.451,
    "add_ffn": 3.915, "store": 3.915,}


def over_lanes(eng, slots, stages):
    order = sorted((k + slots[name], k, n) for n, name in enumerate(stages) for k in range(1 - LANES, LANES)
                   if 0 <= k + slots[name] < LANES)
    run = list(stages.values())

    def turn(i):
        for _, k, n in order:
            t = LANES * i + k
            if not isinstance(t, int) or 0 <= t < NT:
                run[n](t, k % LANES)
    turn(0)
    turn(1)
    with eng.Fori(2, NT // LANES) as i:
        turn(i)
    turn(NT // LANES)


def layer0(nc, a, X, mask, ident, neghalf, x_tile, ps, bufs):
    posT, Y, lanes, xn, xnT, small, jmask, ones = bufs
    ctx = ExitStack()
    with ctx:
        def sb(name, shape, dt=F32):
            return ctx.enter_context(nc.sbuf_tensor(name, shape, dt))

        def sem(name):
            return ctx.enter_context(nc.semaphore(name))

        w_qkv = sb("w_qkv", [P, DC, AQ + 2 * AKV])
        w_o = sb("w_o", [P, AG, D])
        w_ffn = sb("w_ffn", [P, DC, D])
        loraA = sb("loraA", [P, DC, NLR])
        loraB = sb("loraB", [BIAS_ROW + 1, D])
        cos = sb("cos", [P, AD])
        sin = sb("sin", [P, AD])
        causal = sb("causal", [P, L])
        block16 = sb("block16", [P, AKVH])
        starts_i = sb("starts_i", [NLR, 4], I32)
        starts = sb("starts", [NLR, 4])
        batches = sb("batches", [NLR, B])
        chosen = sb("chosen", [NLR, 1])
        reached = sb("reached", [NLR, B])
        adapter = sb("adapter", [NLR, B])
        lora_t = sb("lora_t", [BIAS_ROW + 1, LANES, P])
        QT = sb("lane_QT", [P, LANES, TB, P])
        Vd = sb("lane_Vd", [P, LANES, AKVH, TB, AD + 1])
        gate = sb("gate0", [P, 1])

        w_in = sem("l0_w_in")
        zero_done = sem("l0_zero_done")
        ones_done = sem("l0_ones_done")
        lora_step = sem("lora_step")
        n1, n2, n3 = norm_sems(sem, "n1"), norm_sems(sem, "n2"), norm_sems(sem, "n3")
        names = ("qkv_filled", "cos_done", "rope_terms", "roped", "v_spread", "qk_turned", "qt_ready", "kd_ready",
                 "s_filled", "s_masked", "max_done", "s_shifted", "p_ready", "pt_filled", "pt_ready", "av_filled",
                 "rinv_ready", "o_ready", "ot_filled", "ot_ready", "proj_filled", "proj_added", "lora_filled",
                 "lora_ready", "ffn_filled", "ffn_added", "crucial_ready", "rest_ready", "reduced")
        s = {k: sem(f"l0_{k}") for k in names}

        terms = lambda u: lanes[:, u, 0, 0:QKH * AD]
        roped = lambda u: lanes[:, u, 1, 0:QKH * AD]
        Kd = lambda u: lanes[:, u, 0].rearrange("p (j g k) -> p j g k", j=TB, g=AKVH)
        sm = lambda u: lanes[:, u, 0]
        probs = lambda u: lanes[:, u, 1]
        pT = lambda u: lanes[:, u, 0]
        O = lambda u: xn[:, u]
        OT = lambda u: xnT[:, u]
        crucial = lambda u: lanes[:, u, 0, 0:D]
        rest = lambda u: lanes[:, u, 0, D:2 * D]
        low = lambda u: ps[:, u, 0:512]
        high = lambda u: ps[:, u, 512:1024]

        block = ctx.enter_context(nc.Block())

        @block.sync
        def _(sp):
            n = 0
            for dst, name in ((w_qkv[:], "w_qkv0"), (cos[:], "cos"), (sin[:], "sin"), (causal[:], "causal"),
                              (block16[:], "block16"), (jmask[:], "jmask"), (w_o[:], "w_o0"), (w_ffn[:], "w_ffn0"),
                              (loraA[:], "loraA"), (batches[:], "batches"), (chosen[:], "chosen")):
                sp.dma_start(dst, a[name]).then_inc(w_in, 16)
                n += 1
            sp.dma_start(starts_i[:], a["starts"].rearrange("(o n) -> o n", o=1).to_broadcast([NLR, 4])).then_inc(w_in, 16)
            sp.dma_start(loraB[BIAS_ROW:BIAS_ROW + 1, :], a["ffn_bias"].rearrange("(o n) -> o n", o=1)).then_inc(w_in, 16)
            sp.wait_ge(zero_done, 1)
            sp.dma_start(loraB[0:NLR, :], a["loraB"]).then_inc(w_in, 16)
            assert n + 3 == L0_LOADS

        @block.gpsimd
        def _(pool):
            pool.memset(loraB[0:BIAS_ROW, :], 0.0).then_inc(zero_done, 1)
            pool.wait_ge(zero_done, 1)
            pool.memset(lora_t[0:BIAS_ROW], 0.0).then_inc(zero_done, 1)
            pool.wait_ge(zero_done, 2)
            pool.memset(lora_t[BIAS_ROW:BIAS_ROW + 1], 1.0).then_inc(zero_done, 1)
            pool.wait_ge(zero_done, 3)
            pool.memset(Vd[:], 0.0).then_inc(zero_done, 1)
            pool.wait_ge(zero_done, 4)
            pool.memset(ones[:], 1.0).then_inc(ones_done, 1)
            for j in range(TB):
                pool.wait_ge(ones_done, 1 + j)
                pool.memset(Vd[L * j:L * j + L, :, :, j, AD:AD + 1], 1.0).then_inc(ones_done, 1)
            pool.wait_ge(ones_done, 1 + TB)

            def rope_sum(t, u):
                pool.wait_ge(s["rope_terms"], t + 1)
                pool.tensor_tensor(roped(u), roped(u), terms(u), ALU.add).then_inc(s["roped"], 1)

            def shift(t, u):
                pool.wait_ge(s["max_done"], t + 1)
                v = sm(u).rearrange("p (n k) -> p n k", k=L)
                pool.tensor_tensor(v, v, small["rmax"][:, u].unsqueeze(2).to_broadcast([P, 32, L]), ALU.subtract)\
                    .then_inc(s["s_shifted"], 1)

            def rest_features(t, u):
                pool.wait_ge(s["crucial_ready"], t + 1)
                pool.tensor_tensor(rest(u).rearrange("p (c n) -> p c n", c=DC), posT[:, :, bass.ts(t, P)],
                                   crucial(u).rearrange("p (c n) -> p c n", c=DC), ALU.subtract)\
                    .then_inc(s["rest_ready"], 1)

            over_lanes(pool, SLOTS0, {
                "rstd1": lambda t, u: norm_rstd(pool, n1, t, u, small, neghalf), "rope_sum": rope_sum, "shift": shift,
                "rstd2": lambda t, u: norm_rstd(pool, n2, t, u, small, neghalf),
                "rstd3": lambda t, u: norm_rstd(pool, n3, t, u, small, neghalf), "rest": rest_features})

        @block.tensor
        def _(pe):
            def first_turn(t, u):
                wait(pe, n3["xnT"], t - LANES + 1)
                norm_turn(pe, n1, t, u, xn, high(u), ident)

            def qkv(t, u):
                pe.wait_ge(n1["xnT"], t + 1)
                wait(pe, s["ffn_added"], t - LANES + 1)
                for c in range(DC):
                    pe.matmul(low(u), xnT[:, u, c], w_qkv[:, c, 0:AQ], start=(c == 0), stop=(c == DC - 1))
                for c in range(DC):
                    mm = pe.matmul(high(u)[:, 0:2 * AKV], xnT[:, u, c], w_qkv[:, c, AQ:], start=(c == 0),
                                   stop=(c == DC - 1))
                mm.then_inc(s["qkv_filled"], 1)

            def turn_qk(t, u):
                pe.wait_ge(s["roped"], t + 1)
                pe.wait_ge(s["v_spread"], t + 1)
                for n in range(AG + 1):
                    mm = pe.transpose(ps[:, u, P * n:P * n + P], roped(u)[:, P * n:P * n + P], ident[:])
                mm.then_inc(s["qk_turned"], 1)

            def scores(t, u):
                pe.wait_ge(s["qt_ready"], t + 1)
                pe.wait_ge(s["kd_ready"], t + 1)
                for j in range(TB):
                    mm = pe.matmul(ps[:, u, 256 * j:256 * j + 256], QT[:, u, j], Kd(u)[:, j], start=True, stop=True)
                mm.then_inc(s["s_filled"], 1)

            def turn_probs(t, u):
                pe.wait_ge(s["p_ready"], t + 1)
                for g in range(AKVH):
                    mm = pe.transpose(ps[:, u, P * g:P * g + P], probs(u)[:, P * g:P * g + P], ident[:])
                mm.then_inc(s["pt_filled"], 1)

            def values(t, u):
                pe.wait_ge(s["pt_ready"], t + 1)
                w = TB * (AD + 1)
                for g in range(AKVH):
                    at = 512 * (g // 4) + w * (g % 4)
                    mm = pe.matmul(ps[:, u, at:at + w], pT(u)[:, P * g:P * g + P], Vd[:, u, g], start=True, stop=True)
                mm.then_inc(s["av_filled"], 1)

            def turn_out(t, u):
                pe.wait_ge(s["o_ready"], t + 1)
                for j in range(TB):
                    mm = pe.transpose(high(u)[:, P * j:P * j + P], O(u)[:, P * j:P * j + P], ident[:])
                mm.then_inc(s["ot_filled"], 1)

            def project(t, u):
                pe.wait_ge(s["ot_ready"], t + 1)
                for r in range(AG):
                    mm = pe.matmul(low(u), OT(u)[:, r], w_o[:, r], start=(r == 0), stop=(r == AG - 1))
                mm.then_inc(s["proj_filled"], 1)

            def lora_down(t, u):
                pe.wait_ge(n2["xnT"], t + 1)
                for c in range(DC):
                    mm = pe.matmul(high(u)[0:NLR, 0:P], loraA[:, c], xnT[:, u, c], start=(c == 0), stop=(c == DC - 1))
                mm.then_inc(s["lora_filled"], 1)

            def ffn(t, u):
                for c in range(DC):
                    pe.matmul(low(u), xnT[:, u, c], w_ffn[:, c], start=(c == 0), stop=False)

            def lora_up(t, u):
                pe.wait_ge(s["lora_ready"], t + 1)
                pe.matmul(low(u), lora_t[:, u], loraB[:], start=False, stop=True).then_inc(s["ffn_filled"], 1)

            pe.wait_ge(w_in, 16 * L0_LOADS)
            pe.wait_ge(ones_done, 1 + TB)
            pe.wait_ge(lora_step, 6)
            over_lanes(pe, SLOTS0, {
                "turn1": first_turn, "qkv": qkv, "turn_qk": turn_qk, "scores": scores, "turn_probs": turn_probs,
                "values": values, "turn_out": turn_out, "project": project,
                "turn2": lambda t, u: norm_turn(pe, n2, t, u, xn, high(u), ident), "lora_down": lora_down, "ffn": ffn,
                "lora_up": lora_up, "turn3": lambda t, u: norm_turn(pe, n3, t, u, xn, high(u), ident)})

        @block.scalar
        def _(act):
            def evac_xnT(n):
                def stage(t, u):
                    act.wait_ge(n["xt"], t + 1)
                    act.activation(xnT[:, u].rearrange("p c q -> p (c q)"), high(u), ACT.Copy).then_inc(n["xnT"], 1)
                return stage

            def spread_v(t, u):
                act.wait_ge(s["rope_terms"], t + 1)
                for j in range(TB):
                    rows = slice(L * j, L * j + L)
                    ins = act.activation(Vd[rows, u, :, j, 0:AD],
                                         high(u)[rows, AKV:2 * AKV].rearrange("p (g d) -> p g d", g=AKVH), ACT.Copy)
                ins.then_inc(s["v_spread"], 1)

            def evac_q(t, u):
                act.wait_ge(s["qk_turned"], t + 1)
                act.activation(QT[:, u].rearrange("p j (r q) -> p r j q", r=AG),
                               low(u).rearrange("p (r j q) -> p r j q", r=AG, j=TB), ACT.Copy).then_inc(s["qt_ready"], 1)

            def exps(t, u):
                act.wait_ge(s["s_shifted"], t + 1)
                act.activation(probs(u).rearrange("p (g j k) -> p j g k", g=AKVH, j=TB),
                               sm(u).rearrange("p (j g k) -> p j g k", j=TB, g=AKVH), ACT.Exp, scale=ASCALE)\
                    .then_inc(s["p_ready"], 1)

            def evac_pt(t, u):
                act.wait_ge(s["p_ready"], t + 1)
                act.wait_ge(s["pt_filled"], t + 1)
                act.activation(pT(u), ps[:, u, :], ACT.Copy).then_inc(s["pt_ready"], 1)

            def evac_ot(t, u):
                act.wait_ge(s["ot_filled"], t + 1)
                act.activation(OT(u).rearrange("p r (j q) -> p j r q", j=TB),
                               high(u).rearrange("p (j r q) -> p j r q", j=TB, r=AG), ACT.Copy).then_inc(s["ot_ready"], 1)

            def evac_pos(t, u):
                act.wait_ge(n3["xt"], t + 1)
                act.activation(posT[:, :, bass.ts(t, P)], high(u).rearrange("p (c n) -> p c n", c=DC), ACT.Copy)\
                    .then_inc(n3["xnT"], 1)

            act.wait_ge(ones_done, 1 + TB)
            over_lanes(act, SLOTS0, {"xnT1": evac_xnT(n1), "spread_v": spread_v, "evac_q": evac_q, "exps": exps,
                                     "evac_pt": evac_pt, "evac_ot": evac_ot, "xnT2": evac_xnT(n2), "pos": evac_pos})

        @block.vector
        def _(dve):
            def stats(n, before):
                def stage(t, u):
                    norm_stats(dve, n, t, u, x_tile(t), small, gate, lambda: before(t))
                return stage

            def rows(n):
                return lambda t, u: norm_rows(dve, n, t, u, x_tile(t), small, xn)

            def rope(t, u):
                dve.wait_ge(s["qkv_filled"], t + 1)
                wait(dve, s["reduced"], t - LANES + 1)
                wait(dve, s["rest_ready"], t - LANES + 1)
                src = ps[:, u, 0:QKH * AD].rearrange("p (n d) -> p n d", d=AD)
                half = AD // 2
                dve.tensor_tensor(terms(u).rearrange("p (n d) -> p n d", d=AD), src,
                                  cos[:].unsqueeze(1).to_broadcast([P, QKH, AD]), ALU.mult)
                dst = roped(u).rearrange("p (n d) -> p n d", d=AD)
                for h in range(2):
                    ins = dve.tensor_tensor(dst[:, :, half * h:half * h + half], src[:, :, half * (1 - h):half * (2 - h)],
                                            sin[:, half * h:half * h + half].unsqueeze(1).to_broadcast([P, QKH, half]),
                                            ALU.mult)
                ins.then_inc(s["rope_terms"], 1)

            def spread_k(t, u):
                dve.wait_ge(s["qk_turned"], t + 1)
                for j in range(TB):
                    ins = dve.tensor_tensor(Kd(u)[:, j],
                                            high(u)[:, L * j:L * j + L].unsqueeze(1).to_broadcast([P, AKVH, L]),
                                            block16[:].unsqueeze(2).to_broadcast([P, AKVH, L]), ALU.mult)
                ins.then_inc(s["kd_ready"], 1)

            def mask_scores(t, u):
                dve.wait_ge(s["s_filled"], t + 1)
                v = sm(u).rearrange("p (n k) -> p n k", k=L)
                dve.tensor_tensor(v, ps[:, u, :].rearrange("p (n k) -> p n k", k=L),
                                  causal[:].unsqueeze(1).to_broadcast([P, 32, L]), ALU.add).then_inc(s["s_masked"], 1)
                dve.wait_ge(s["s_masked"], t + 1)
                dve.tensor_reduce(small["rmax"][:, u], v, AX.X, ALU.max).then_inc(s["max_done"], 1)

            def normalise(t, u):
                dve.wait_ge(s["av_filled"], t + 1)
                src = ps[:, u, :].rearrange("p (a n) -> p a n", a=2)[:, :, 0:4 * TB * (AD + 1)]\
                    .rearrange("p a (g j d) -> p a g j d", g=4, j=TB)
                rinv = small["rinv"][:, u].rearrange("p (a g j) -> p a g j", a=2, g=4)
                dve.reciprocal(rinv, src[:, :, :, :, AD]).then_inc(s["rinv_ready"], 1)
                dve.wait_ge(s["rinv_ready"], t + 1)
                dst = O(u).rearrange("p (j a g d) -> p a g j d", j=TB, a=2, g=4)
                for h in range(2):
                    ins = dve.tensor_tensor(dst[:, h], src[:, h, :, :, 0:AD],
                                            rinv[:, h].unsqueeze(3).to_broadcast([P, 4, TB, AD]), ALU.mult)
                ins.then_inc(s["o_ready"], 1)

            def add_projected(t, u):
                dve.wait_ge(s["proj_filled"], t + 1)
                dve.tensor_tensor(x_tile(t), x_tile(t), low(u), ALU.add).then_inc(s["proj_added"], 1)

            def lora_mask(t, u):
                dve.wait_ge(s["lora_filled"], t + 1)
                wait(dve, s["ffn_filled"], t - LANES + 1)
                dve.tensor_tensor(lora_t[0:NLR, u].rearrange("p (j q) -> p j q", j=TB),
                                  high(u)[0:NLR, 0:P].rearrange("p (j q) -> p j q", j=TB),
                                  adapter[:, bass.ts(t, TB)].unsqueeze(2).to_broadcast([NLR, TB, L]), ALU.mult)\
                    .then_inc(s["lora_ready"], 1)

            def add_ffn(t, u):
                dve.wait_ge(s["ffn_filled"], t + 1)
                dve.tensor_tensor(x_tile(t), x_tile(t), low(u), ALU.add).then_inc(s["ffn_added"], 1)

            def crucial_features(t, u):
                dve.wait_ge(n3["xnT"], t + 1)
                dve.tensor_tensor(crucial(u).rearrange("p (c n) -> p c n", c=DC), posT[:, :, bass.ts(t, P)],
                                  mask[:, :, bass.ts(t, P)], ALU.mult).then_inc(s["crucial_ready"], 1)

            def reduce_channels(t, u):
                dve.wait_ge(s["rest_ready"], t + 1)
                for which, part in ((0, crucial(u)), (1, rest(u))):
                    src = part.rearrange("p (c j n) -> p c j n", c=DC, j=TB)
                    for kind, op in ((0, ALU.max), (1, ALU.add)):
                        ins = dve.tensor_reduce(Y[:, :, kind, which, bass.ts(t, TB)], src, AX.X, op)
                ins.then_inc(s["reduced"], 1)

            dve.wait_ge(w_in, 16 * L0_LOADS)
            dve.tensor_copy(starts[:], starts_i[:]).then_inc(lora_step, 1)
            dve.wait_ge(lora_step, 1)
            dve.tensor_scalar(reached[:], batches[:], starts[:, 0:1], None, ALU.is_ge).then_inc(lora_step, 1)
            for k in range(1, 4):
                dve.wait_ge(lora_step, k + 1)
                dve.scalar_tensor_tensor(out=reached[:], in0=batches[:], scalar=starts[:, k:k + 1], in1=reached[:],
                                         op0=ALU.is_ge, op1=ALU.add).then_inc(lora_step, 1)
            dve.wait_ge(lora_step, 5)
            dve.tensor_scalar(adapter[:], reached[:], chosen[:, 0:1], None, ALU.is_equal).then_inc(lora_step, 1)
            dve.wait_ge(lora_step, 6)
            dve.wait_ge(zero_done, 4)

            def before1(t):
                wait(dve, n3["xt"], t - LANES + 1)

            def before2(t):
                dve.wait_ge(s["proj_added"], t + 1)

            def before3(t):
                dve.wait_ge(s["ffn_added"], t + 1)

            over_lanes(dve, SLOTS0, {
                "stats1": stats(n1, before1), "rows1": rows(n1), "rope": rope, "spread_k": spread_k,
                "mask": mask_scores, "normalise": normalise, "add_proj": add_projected, "stats2": stats(n2, before2),
                "rows2": rows(n2), "lora_mask": lora_mask, "add_ffn": add_ffn, "stats3": stats(n3, before3),
                "rows3": rows(n3), "crucial": crucial_features, "reduce": reduce_channels})


def mix_gates(nc, a, neghalf, ps, Y, ones, blend):
    ctx = ExitStack()
    with ctx:
        def sb(name, shape, dt=F32):
            return ctx.enter_context(nc.sbuf_tensor(name, shape, dt))

        def sem(name):
            return ctx.enter_context(nc.semaphore(name))

        shifted = sb("shifted", [P, 3 * P + TAPS - 1])
        taps = sb("taps", [P, 2 * TAPS])
        affine = sb("affine", [P, 2])
        band = sb("band", [P, 2, 3 * P])
        Z = sb("Z", [P, DC, 2, B])
        sq = sb("sq", [P, DC, 2, B])
        part = sb("part", [P, 2])
        moment = sb("moment", [P, 2])
        rstd = sb("mix_rstd", [P, 2])
        c_in, step, band_step = sem("mix_c_in"), sem("mix_step"), sem("band_step")
        conv_done, sums_done, pow_done = sem("conv_done"), sem("sums_done"), sem("mix_pow_done")
        sig_done = sem("sig_done")
        conv = ps[:, 0, 0:DC * 2 * B]
        sums = ps[:, 1, 0:2]
        sums2 = ps[:, 2, 0:2]
        block = ctx.enter_context(nc.Block())
        count = float(B * D)
        by_which = "p c w b -> p w c b"

        @block.sync
        def _(sp):
            sp.dma_start(shifted[:], a["shifted"]).then_inc(c_in, 16)
            sp.dma_start(taps[:], a["taps"].rearrange("(o n) -> o n", o=1).to_broadcast([P, 2 * TAPS])).then_inc(c_in, 16)
            sp.dma_start(affine[:, 0:1], a["bn_gamma"].rearrange("(o n) -> o n", o=1).to_broadcast([P, 1])).then_inc(c_in, 16)
            sp.dma_start(affine[:, 1:2], a["bn_beta"].rearrange("(o n) -> o n", o=1).to_broadcast([P, 1])).then_inc(c_in, 16)

        @block.tensor
        def _(pe):
            pe.wait_ge(band_step, 2 * TAPS + 2)
            for o in range(DC):
                pairs = [(i, ch) for i in (o - 1, o, o + 1) if 0 <= i < DC for ch in range(2)]
                for n, (i, ch) in enumerate(pairs):
                    at = P * (o - i + 1)
                    mm = pe.matmul(conv[:, 2 * B * o:2 * B * (o + 1)], band[:, ch, at:at + P],
                                   Y[:, i, ch].rearrange("p w b -> p (w b)"), start=(n == 0), stop=(n == len(pairs) - 1))
            mm.then_inc(conv_done, 1)
            pe.wait_ge(step, 2)
            pe.matmul(sums, ones[:], part[:], start=True, stop=True).then_inc(sums_done, 1)
            pe.wait_ge(step, 6)
            pe.matmul(sums2, ones[:], part[:], start=True, stop=True).then_inc(sums_done, 1)

        @block.gpsimd
        def _(pool):
            pool.wait_ge(step, 7)
            for w in range(2):
                ins = pool.tensor_tensor(rstd[:, w:w + 1], moment[:, w:w + 1], neghalf[:], ALU.pow)
            ins.then_inc(pow_done, 1)

        @block.scalar
        def _(act):
            act.wait_ge(step, 9)
            act.activation(Z[:].rearrange("p c w b -> p (c w b)"), Z[:].rearrange("p c w b -> p (c w b)"),
                           ACT.Sigmoid).then_inc(sig_done, 1)

        @block.vector
        def _(dve):
            dve.tensor_scalar(Y[:, :, 1, 0, :], Y[:, :, 1, 0, :], 1.0 / L, float(L / TOPK), ALU.mult, ALU.mult)\
                .then_inc(band_step, 1)
            dve.tensor_scalar(Y[:, :, 1, 1, :], Y[:, :, 1, 1, :], 1.0 / L, float(L / (L - TOPK)), ALU.mult, ALU.mult)\
                .then_inc(band_step, 1)
            dve.wait_ge(c_in, 64)
            n = 2
            for tap in range(TAPS):
                for ch in range(2):
                    w = taps[:, TAPS * ch + tap:TAPS * ch + tap + 1]
                    src = shifted[:, tap:tap + 3 * P]
                    if tap == 0:
                        ins = dve.tensor_scalar(band[:, ch], src, w, None, ALU.mult)
                    else:
                        dve.wait_ge(band_step, n - 1)
                        ins = dve.scalar_tensor_tensor(out=band[:, ch], in0=src, scalar=w, in1=band[:, ch],
                                                       op0=ALU.mult, op1=ALU.add)
                    ins.then_inc(band_step, 1)
                    n += 1
            dve.wait_ge(conv_done, 1)
            z = Z[:].rearrange("p c w b -> p (c w b)")
            dve.tensor_copy(z, conv).then_inc(step, 1)
            dve.wait_ge(step, 1)
            dve.tensor_reduce(part[:], Z[:].rearrange(by_which), AX.XY, ALU.add).then_inc(step, 1)
            dve.wait_ge(sums_done, 1)
            dve.tensor_scalar(moment[:], sums, 1.0 / count, None, ALU.mult).then_inc(step, 1)
            dve.wait_ge(step, 3)
            dve.tensor_tensor(Z[:].rearrange("p c w b -> p c w b"), Z[:],
                              moment[:].unsqueeze(1).unsqueeze(3).to_broadcast([P, DC, 2, B]), ALU.subtract)\
                .then_inc(step, 1)
            dve.wait_ge(step, 4)
            dve.tensor_tensor(sq[:], Z[:], Z[:], ALU.mult).then_inc(step, 1)
            dve.wait_ge(step, 5)
            dve.tensor_reduce(part[:], sq[:].rearrange(by_which), AX.XY, ALU.add).then_inc(step, 1)
            dve.wait_ge(sums_done, 2)
            dve.tensor_scalar(moment[:], sums2, 1.0 / count, EPS, ALU.mult, ALU.add).then_inc(step, 1)
            dve.wait_ge(pow_done, 1)
            dve.tensor_tensor(Z[:], Z[:], rstd[:].unsqueeze(1).unsqueeze(3).to_broadcast([P, DC, 2, B]), ALU.mult)\
                .then_inc(band_step, 1)
            dve.wait_ge(band_step, n + 1)
            dve.tensor_scalar(z, z, affine[:, 0:1], affine[:, 1:2], ALU.mult, ALU.add).then_inc(step, 1)
            dve.wait_ge(step, 8)
            dve.tensor_scalar(z, z, 0.0, None, ALU.max).then_inc(step, 1)
            dve.wait_ge(sig_done, 1)
            dve.tensor_copy(blend[:, :, 0, :], Z[:, :, 1, :])
            dve.tensor_tensor(blend[:, :, 1, :], Z[:, :, 0, :], Z[:, :, 1, :], ALU.subtract)


def layer1(nc, a, X, mask, ident, neghalf, x_tile, ps, bufs, blend):
    posT, Y, lanes, xn, xnT, small, jmask, ones = bufs
    ctx = ExitStack()
    with ctx:
        def sb(name, shape, dt=F32):
            return ctx.enter_context(nc.sbuf_tensor(name, shape, dt))

        def sem(name):
            return ctx.enter_context(nc.semaphore(name))

        w_qkv = sb("w_qkv1", [P, DC, 3 * EW])
        w_o = sb("w_o1", [P, EW // P, D])
        w_ffn = sb("w_ffn1", [P, DC, D])
        ffn_mask = sb("ffn_mask", [P, DC, D], U8)
        b_qk = sb("b_qk", [P, 4])
        b_v = sb("b_v", [P, EW])
        b_o = sb("b_o", [P, D])
        keep = sb("keep", [P, 2, L])
        QK = sb("lane_QK", [P, LANES, 4, P])
        V = sb("lane_V", [P, LANES, EW])
        p = sb("lane_p", [P, LANES, EW])
        gate = sb("gate1", [P, 1])

        w_in, w_ready = sem("l1_w_in"), sem("l1_w_ready")
        n4, n5 = norm_sems(sem, "n4"), norm_sems(sem, "n5")
        names = ("gated", "gate_added", "mixed", "mix_turned", "mix_added", "bias_added", "qkv_filled", "v_ready",
                 "qk_ready", "kd_ready", "s_filled", "s_kept", "s_masked", "max_done", "s_shifted", "p_ready",
                 "sum_done", "rinv_ready", "pd_ready", "pt_filled", "pt_ready", "av_filled", "o_ready", "ot_filled",
                 "ot_ready", "proj_filled", "proj_added", "ffn_filled", "ffn_added")
        s = {k: sem(f"l1_{k}") for k in names}
        out_done = sem("out_done")

        mixed = lambda u: lanes[:, u, 0, 0:D]
        Kd = lambda u: lanes[:, u, 0].rearrange("p (a j h k) -> p a j h k", a=2, j=TB, h=4)
        Pd = lambda u: lanes[:, u, 0].rearrange("p (h j k) -> p h j k", h=EH, j=TB)
        pT = lambda u: lanes[:, u, 1]
        O = lambda u: xn[:, u, 0:EW]
        OT = lambda u: xnT[:, u, 0:EW // P]
        low = lambda u: ps[:, u, 0:512]
        high = lambda u: ps[:, u, 512:1024]
        loads = 9

        block = ctx.enter_context(nc.Block())

        @block.sync
        def _(sp):
            row = lambda x, n: x.rearrange("(o n) -> o n", o=1).to_broadcast([P, n])
            sp.dma_start(w_ffn[:], a["w_ffn1"]).then_inc(w_in, 16)
            sp.dma_start(ffn_mask[:], a["ffn_mask"]).then_inc(w_in, 16)
            sp.dma_start(w_qkv[:], a["w_qkv1"]).then_inc(w_in, 16)
            sp.dma_start(w_o[:], a["w_o1"]).then_inc(w_in, 16)
            sp.dma_start(b_qk[:], a["b_qk1"]).then_inc(w_in, 16)
            sp.dma_start(b_v[:], row(a["b_v1"], EW)).then_inc(w_in, 16)
            sp.dma_start(b_o[:], row(a["b_o1"], D)).then_inc(w_in, 16)
            sp.dma_start(keep[:, 0], a["keep1"]).then_inc(w_in, 16)
            sp.dma_start(keep[:, 1], a["masked1"]).then_inc(w_in, 16)

            def store(t, u):
                sp.wait_ge(s["ffn_added"], t + 1)
                if isinstance(t, int):
                    sp.dma_start(a["y"][t], x_tile(t)).then_inc(out_done, 16)
                else:
                    sp.dma_start(a["y"][bass.ds(t, 1)].rearrange("a p d -> (a p) d"), x_tile(t)).then_inc(out_done, 16)

            over_lanes(sp, SLOTS1, {"store": store})
            sp.wait_ge(out_done, 16 * NT)

        @block.gpsimd
        def _(pool):
            pool.wait_ge(w_in, 16 * loads)

            def add_rest(t, u):
                pool.wait_ge(s["gated"], t + 1)
                v = mixed(u).rearrange("p (c j n) -> p c j n", c=DC, j=TB)
                for c in range(DC):
                    ins = pool.tensor_tensor(v[:, c], v[:, c],
                                             blend[:, c, 0, bass.ts(t, TB)].unsqueeze(2).to_broadcast([P, TB, L]), ALU.add)
                ins.then_inc(s["gate_added"], 1)

            def bias_rows(t, u):
                pool.wait_ge(n4["xn"], t + 1)
                pool.tensor_tensor(x_tile(t), x_tile(t), b_o[:], ALU.add).then_inc(s["bias_added"], 1)

            def spread_k(t, u):
                pool.wait_ge(s["qk_ready"], t + 1)
                for half in range(2):
                    for j in range(TB):
                        ins = pool.tensor_tensor(Kd(u)[:, half, j],
                                                 QK[:, u, 2 + half, L * j:L * j + L].unsqueeze(1).to_broadcast([P, 4, L]),
                                                 jmask[:].unsqueeze(2).to_broadcast([P, 4, L]), ALU.mult)
                ins.then_inc(s["kd_ready"], 1)

            def shift(t, u):
                pool.wait_ge(s["max_done"], t + 1)
                v = p[:, u].rearrange("p (h k) -> p h k", h=EH)
                pool.tensor_tensor(v, v, small["rmax"][:, u, 0:EH].unsqueeze(2).to_broadcast([P, EH, L]), ALU.subtract)\
                    .then_inc(s["s_shifted"], 1)

            over_lanes(pool, SLOTS1, {
                "add_rest": add_rest, "rstd1": lambda t, u: norm_rstd(pool, n4, t, u, small, neghalf),
                "bias": bias_rows, "spread_k": spread_k, "shift": shift,
                "rstd2": lambda t, u: norm_rstd(pool, n5, t, u, small, neghalf)})

        @block.tensor
        def _(pe):
            def turn_mix(t, u):
                pe.wait_ge(s["mixed"], t + 1)
                wait(pe, s["ffn_added"], t - LANES + 1)
                for c in range(DC):
                    mm = pe.transpose(low(u)[:, P * c:P * c + P], mixed(u)[:, P * c:P * c + P], ident[:])
                mm.then_inc(s["mix_turned"], 1)

            def qkv(t, u):
                pe.wait_ge(n4["xnT"], t + 1)
                for n in range(4):
                    for c in range(DC):
                        pe.matmul(low(u)[:, P * n:P * n + P], w_qkv[:, c, P * n:P * n + P], xnT[:, u, c],
                                  start=(c == 0), stop=(c == DC - 1))
                for c in range(DC):
                    mm = pe.matmul(high(u)[:, 0:EW], xnT[:, u, c], w_qkv[:, c, 2 * EW:], start=(c == 0), stop=(c == DC - 1))
                mm.then_inc(s["qkv_filled"], 1)

            def scores(t, u):
                pe.wait_ge(s["qk_ready"], t + 1)
                pe.wait_ge(s["kd_ready"], t + 1)
                for half in range(2):
                    for j in range(TB):
                        mm = pe.matmul(low(u)[L * j:L * j + L, P * half:P * half + P], QK[:, u, half, L * j:L * j + L],
                                       Kd(u)[:, half, j], start=True, stop=True, tile_position=(0, L * j))
                mm.then_inc(s["s_filled"], 1)

            def turn_probs(t, u):
                pe.wait_ge(s["pd_ready"], t + 1)
                pe.wait_ge(s["v_ready"], t + 1)
                for h in range(EH):
                    mm = pe.transpose(ps[:, u, P * h:P * h + P], Pd(u)[:, h].rearrange("p j k -> p (j k)"), ident[:])
                mm.then_inc(s["pt_filled"], 1)

            def values(t, u):
                pe.wait_ge(s["pt_ready"], t + 1)
                for h in range(EH):
                    mm = pe.matmul(low(u)[:, L * h:L * h + L], pT(u)[:, P * h:P * h + P], V[:, u, L * h:L * h + L],
                                   start=True, stop=True)
                mm.then_inc(s["av_filled"], 1)

            def turn_out(t, u):
                pe.wait_ge(s["o_ready"], t + 1)
                for n in range(EW // P):
                    mm = pe.transpose(high(u)[:, P * n:P * n + P], O(u)[:, P * n:P * n + P], ident[:])
                mm.then_inc(s["ot_filled"], 1)

            def project(t, u):
                pe.wait_ge(s["ot_ready"], t + 1)
                for n in range(EW // P):
                    mm = pe.matmul(low(u), OT(u)[:, n], w_o[:, n], start=(n == 0), stop=(n == EW // P - 1))
                mm.then_inc(s["proj_filled"], 1)

            def ffn(t, u):
                pe.wait_ge(n5["xnT"], t + 1)
                for c in range(DC):
                    mm = pe.matmul(low(u), xnT[:, u, c], w_ffn[:, c], start=(c == 0), stop=(c == DC - 1))
                mm.then_inc(s["ffn_filled"], 1)

            pe.wait_ge(w_ready, 1)
            over_lanes(pe, SLOTS1, {
                "turn_mix": turn_mix, "turn1": lambda t, u: norm_turn(pe, n4, t, u, xn, high(u), ident), "qkv": qkv,
                "scores": scores, "turn_probs": turn_probs, "values": values, "turn_out": turn_out, "project": project,
                "turn2": lambda t, u: norm_turn(pe, n5, t, u, xn, high(u), ident), "ffn": ffn})

        @block.scalar
        def _(act):
            def evac_xnT(n):
                def stage(t, u):
                    act.wait_ge(n["xt"], t + 1)
                    wait(act, s["ffn_filled"], t - LANES + 1)
                    act.activation(xnT[:, u].rearrange("p c q -> p (c q)"), high(u), ACT.Copy).then_inc(n["xnT"], 1)
                return stage

            def evac_qk(t, u):
                act.wait_ge(s["qkv_filled"], t + 1)
                wait(act, s["kd_ready"], t - LANES + 1)
                for n in range(4):
                    ins = act.activation(QK[:, u, n], low(u)[:, P * n:P * n + P], ACT.Identity, bias=b_qk[:, n:n + 1])
                ins.then_inc(s["qk_ready"], 1)

            def exps(t, u):
                act.wait_ge(s["s_shifted"], t + 1)
                act.activation(p[:, u], p[:, u], ACT.Exp).then_inc(s["p_ready"], 1)

            def evac_pt(t, u):
                act.wait_ge(s["pt_filled"], t + 1)
                wait(act, s["av_filled"], t - LANES + 1)
                act.activation(pT(u), ps[:, u, :], ACT.Copy).then_inc(s["pt_ready"], 1)

            def evac_ot(t, u):
                act.wait_ge(s["ot_filled"], t + 1)
                act.activation(OT(u).rearrange("p n q -> p (n q)"), high(u)[:, 0:EW], ACT.Copy).then_inc(s["ot_ready"], 1)

            act.wait_ge(w_in, 16 * loads)
            over_lanes(act, SLOTS1, {"xnT1": evac_xnT(n4), "evac_qk": evac_qk, "exps": exps, "evac_pt": evac_pt,
                                     "evac_ot": evac_ot, "xnT2": evac_xnT(n5)})

        @block.vector
        def _(dve):
            def gate_crucial(t, u):
                wait(dve, s["pt_filled"], t - LANES + 1)
                v = mixed(u).rearrange("p (c j n) -> p c j n", c=DC, j=TB)
                m = mask[:, :, bass.ts(t, P)].rearrange("p c (j n) -> p c j n", j=TB)
                dve.tensor_tensor(v, m, blend[:, :, 1, bass.ts(t, TB)].unsqueeze(3).to_broadcast([P, DC, TB, L]),
                                  ALU.mult).then_inc(s["gated"], 1)

            def mix(t, u):
                dve.wait_ge(s["gate_added"], t + 1)
                v = mixed(u).rearrange("p (c n) -> p c n", c=DC)
                dve.tensor_tensor(v, v, posT[:, :, bass.ts(t, P)], ALU.mult).then_inc(s["mixed"], 1)

            def add_mix(t, u):
                dve.wait_ge(s["mix_turned"], t + 1)
                dve.tensor_tensor(x_tile(t), x_tile(t), low(u), ALU.add).then_inc(s["mix_added"], 1)

            def before4(t):
                dve.wait_ge(s["mix_added"], t + 1)
                wait(dve, n5["xt"], t - LANES + 1)

            def before5(t):
                dve.wait_ge(s["proj_added"], t + 1)

            def stats(n, before):
                def stage(t, u):
                    norm_stats(dve, n, t, u, x_tile(t), small, gate, lambda: before(t))
                return stage

            def rows(n):
                return lambda t, u: norm_rows(dve, n, t, u, x_tile(t), small, xn)

            def evac_v(t, u):
                dve.wait_ge(s["qkv_filled"], t + 1)
                wait(dve, s["av_filled"], t - LANES + 1)
                dve.tensor_tensor(V[:, u], high(u)[:, 0:EW], b_v[:], ALU.add).then_inc(s["v_ready"], 1)

            def mask_scores(t, u):
                dve.wait_ge(s["s_filled"], t + 1)
                v = p[:, u].rearrange("p (h k) -> p h k", h=EH)
                dve.tensor_tensor(v, low(u)[:, 0:EW].rearrange("p (h k) -> p h k", h=EH),
                                  keep[:, 0].unsqueeze(1).to_broadcast([P, EH, L]), ALU.mult).then_inc(s["s_kept"], 1)
                dve.wait_ge(s["s_kept"], t + 1)
                dve.tensor_tensor(v, v, keep[:, 1].unsqueeze(1).to_broadcast([P, EH, L]), ALU.add).then_inc(s["s_masked"], 1)
                dve.wait_ge(s["s_masked"], t + 1)
                dve.tensor_reduce(small["rmax"][:, u, 0:EH], v, AX.X, ALU.max).then_inc(s["max_done"], 1)

            def spread_p(t, u):
                dve.wait_ge(s["p_ready"], t + 1)
                v = p[:, u].rearrange("p (h k) -> p h k", h=EH)
                dve.tensor_reduce(small["rsum"][:, u], v, AX.X, ALU.add).then_inc(s["sum_done"], 1)
                for j in range(TB):
                    ins = dve.tensor_scalar(Pd(u)[:, :, j], v, jmask[:, j:j + 1], None, ALU.mult)
                ins.then_inc(s["pd_ready"], 1)
                dve.wait_ge(s["sum_done"], t + 1)
                dve.reciprocal(small["rinv"][:, u, 0:EH], small["rsum"][:, u]).then_inc(s["rinv_ready"], 1)

            def normalise(t, u):
                dve.wait_ge(s["av_filled"], t + 1)
                dve.wait_ge(s["rinv_ready"], t + 1)
                dve.tensor_tensor(O(u).rearrange("p (h d) -> p h d", h=EH), low(u)[:, 0:EW].rearrange("p (h d) -> p h d", h=EH),
                                  small["rinv"][:, u, 0:EH].unsqueeze(2).to_broadcast([P, EH, L]), ALU.mult)\
                    .then_inc(s["o_ready"], 1)

            def add_projected(t, u):
                dve.wait_ge(s["proj_filled"], t + 1)
                dve.wait_ge(s["bias_added"], t + 1)
                dve.tensor_tensor(x_tile(t), x_tile(t), low(u), ALU.add).then_inc(s["proj_added"], 1)

            def add_ffn(t, u):
                dve.wait_ge(s["ffn_filled"], t + 1)
                dve.tensor_tensor(x_tile(t), x_tile(t), low(u), ALU.add).then_inc(s["ffn_added"], 1)

            dve.wait_ge(w_in, 16 * loads)
            dve.tensor_tensor(w_ffn[:], w_ffn[:], ffn_mask[:], ALU.mult).then_inc(w_ready, 1)
            over_lanes(dve, SLOTS1, {
                "gate": gate_crucial, "mix": mix, "add_mix": add_mix, "stats1": stats(n4, before4), "rows1": rows(n4),
                "evac_v": evac_v, "mask": mask_scores, "spread_p": spread_p, "normalise": normalise,
                "add_proj": add_projected, "stats2": stats(n5, before5), "rows2": rows(n5), "add_ffn": add_ffn})


def k_perm():
    return np.concatenate([np.arange(h * HD + lo, h * HD + hi) for h, lo, hi in K_ROWS])


def by_chunks(w):
    return np.ascontiguousarray(w.T.reshape(-1, P, w.shape[0]).transpose(1, 0, 2))


def tables():
    rows = np.arange(P)
    q = rows % L
    freqs = (1.0 / 10000.0 ** (np.arange(0, AD, 2, dtype=np.float32) / np.float32(AD))).astype(np.float32)
    ang = np.outer(q.astype(np.float32), freqs).astype(np.float32)
    cos, sin = np.cos(ang), np.sin(ang)
    later = np.arange(L)[None, :] > q[:, None]
    out = {
        "ident": np.eye(P), "cos": np.concatenate([cos, cos], 1), "sin": np.concatenate([-sin, sin], 1),
        "causal": np.where(later, -1e30, 0.0), "keep1": np.where(later, 0.0, 1.0), "masked1": np.where(later, -10000.0, 0.0),
        "block16": rows[:, None] // AD == np.arange(AKVH)[None, :], "jmask": rows[:, None] // L == np.arange(TB)[None, :],
        "batches": np.broadcast_to(np.arange(B)[None, :], (NLR, B)), "chosen": (np.arange(NLR)[:, None] // 16) + 2,
        "shifted": np.arange(3 * P + TAPS - 1)[None, :] == rows[:, None] + P + TAPS // 2,
    }
    return {k: np.ascontiguousarray(v.astype(np.float32)) for k, v in out.items()}


def lay_out(x, ctx_4096, L0_xattn_Wq, L0_xattn_Wk, L0_xattn_Wv, L0_xattn_Wo, L0_attn_wq, L0_attn_wk, L0_attn_wv,
            L0_attn_wo, L0_ffn_weight, L0_ffn_bias, L0_ffn_lora_A, L0_ffn_lora_B, L0_ffn_lora_start_indices,
            L1_xattn_conv_w, L1_xattn_bn_gamma, L1_xattn_bn_beta, L1_attn_w_qkv, L1_attn_b_qkv, L1_attn_w_o,
            L1_attn_b_o, L1_ffn_W, L1_ffn_mask):
    perm = k_perm()
    c = np.ascontiguousarray
    out = {}
    out["x"] = c(x.reshape(NT, P, D).transpose(1, 0, 2))
    out["ctxT"] = c(ctx_4096.reshape(B, CTX, DC, P).transpose(0, 3, 2, 1))
    out["ctx_last"] = c(ctx_4096[:, CTX - 1, :].reshape(B, DC, P).transpose(2, 1, 0))
    heads, inner = perm // HD, perm % HD
    q_rows = np.concatenate([((heads[P * k:P * k + P] * G + r) * HD + inner[P * k:P * k + P])
                             for k in range(NKT) for r in range(G)])
    out["WqT"] = by_chunks(L0_xattn_Wq[q_rows])
    out["WkT"] = by_chunks(L0_xattn_Wk[perm])
    out["WvT"] = by_chunks(L0_xattn_Wv)
    col = np.arange(KW)
    o_cols = np.concatenate([((col[P * k:P * k + P] // HD) * G + r) * HD + col[P * k:P * k + P] % HD
                             for k in range(NKT) for r in range(G)])
    out["WoT"] = c(L0_xattn_Wo[:, o_cols].T.reshape(NKT * G, P, D).transpose(1, 0, 2))
    halves = np.concatenate([np.arange(0, AD, 2), np.arange(1, AD, 2)])
    k_cols = (np.arange(AKVH)[:, None] * AD + halves[None, :]).ravel()
    q_cols = np.concatenate([((np.arange(AKVH) * AG + r)[:, None] * AD + halves[None, :]).ravel() for r in range(AG)])
    out["w_qkv0"] = by_chunks(np.concatenate([L0_attn_wq[:, q_cols], L0_attn_wk[:, k_cols], L0_attn_wv], 1).T)
    o_rows = np.stack([((np.arange(AKVH) * AG + r)[:, None] * AD + np.arange(AD)[None, :]).ravel() for r in range(AG)])
    out["w_o0"] = c(L0_attn_wo[o_rows].transpose(1, 0, 2))
    out["w_ffn0"] = by_chunks(L0_ffn_weight)
    out["ffn_bias"] = c(L0_ffn_bias)
    out["loraA"] = by_chunks(L0_ffn_lora_A.reshape(NLR, D))
    out["loraB"] = c(L0_ffn_lora_B.transpose(0, 2, 1).reshape(NLR, D))
    out["starts"] = c(L0_ffn_lora_start_indices)
    out["taps"] = c(L1_xattn_conv_w.reshape(-1))
    out["bn_gamma"] = c(L1_xattn_bn_gamma)
    out["bn_beta"] = c(L1_xattn_bn_beta)
    out["w_qkv1"] = by_chunks(L1_attn_w_qkv)
    out["b_qk1"] = c(L1_attn_b_qkv[0:2 * EW].reshape(-1, P).T)
    out["b_v1"] = c(L1_attn_b_qkv[2 * EW:])
    out["w_o1"] = by_chunks(L1_attn_w_o)
    out["b_o1"] = c(L1_attn_b_o)
    out["w_ffn1"] = by_chunks(L1_ffn_W)
    out["ffn_mask"] = by_chunks(L1_ffn_mask)
    out.update(tables())
    return out


def kernel(**inputs):
    import concourse.bacc as bacc
    from concourse.bass_utils import run_bass_kernel_spmd

    nc = bacc.Bacc("TRN2", target_bir_lowering=False, num_devices=1)
    arrays = lay_out(**{k: np.asarray(v) for k, v in inputs.items()})
    a = {k: nc.dram_tensor(f"in_{k}", v.shape, mybir.dt.from_np(v.dtype), kind="ExternalInput").ap()
         for k, v in arrays.items()}
    a["y"] = nc.dram_tensor("y", (NT, P, D), F32, kind="ExternalOutput").ap()
    build_program(nc, a)
    r = run_bass_kernel_spmd(nc, [{f"in_{k}": v for k, v in arrays.items()}], core_ids=[0])
    return r.results[0]["y"].reshape(B, L, D)
```

```python
from contextlib import ExitStack

import numpy as np

import concourse.bass as bass
from concourse import mybir

F32 = mybir.dt.float32
I32 = mybir.dt.int32
U8 = mybir.dt.uint8
ALU = mybir.AluOpType
ACT = mybir.ActivationFunctionType
AX = mybir.AxisListType

P = 128
B, L, D = 64, 32, 512
CTX = 257
DC = D // P
TB = P // L
NT = B // TB
EPS = 1e-5

KVH, G, HD = 4, 4, 96
KW = KVH * HD
NKT = KW // P
S = CTX + L
TAIL = L + 1
XSCALE = 1.0 / float(np.sqrt(np.float32(HD)))
TOPK = 20
GONE = -3.0e38

K_ROWS = [(0, 0, 96), (1, 64, 96), (1, 0, 64), (2, 0, 64), (3, 0, 96), (2, 64, 96)]
PARTS = [(0, 0, 0, 96, 0), (1, 0, 96, 128, 64), (1, 1, 0, 64, 0), (2, 1, 64, 128, 0), (3, 2, 0, 96, 0),
         (2, 2, 96, 128, 64)]


LANES = 4
AKVH, AG, AD = 8, 4, 16
AQ, AKV = AKVH * AG * AD, AKVH * AD
QKH = AKVH * (AG + 1)
ASCALE = 0.25
NLR, BIAS_ROW = 48, 64
EARLY_LOADS, LATE_LOADS = 9, 11
TAPS = 7
EH, EW = 8, 256


def wait(eng, sem, value):
    if not isinstance(value, int) or value > 0:
        eng.wait_ge(sem, value)


def build_program(nc, a):
    ctx = ExitStack()
    with ctx:
        def sb(name, shape, dt=F32):
            return ctx.enter_context(nc.sbuf_tensor(name, shape, dt))

        def sem(name):
            return ctx.enter_context(nc.semaphore(name))

        X = sb("X", [P, NT * D])
        mask = sb("mask", [P, DC, B * L], U8)
        ident = sb("ident", [P, P])
        neghalf = sb("neghalf", [P, 1])
        early = {k: sb(k, shape) for k, shape in (
            ("w_qkv", [P, DC, AQ + 2 * AKV]), ("w_o", [P, AG, D]), ("w_ffn", [P, DC, D]), ("loraA", [P, DC, NLR]),
            ("cos", [P, AD]), ("sin", [P, AD]),
            ("causal", [P, L]),
            ("block16", [P, 4]),
            ("jmask", [P, TB]),
            ("adapter", [NLR, B]),
            ("band", [P, 2, 3 * P]))}
        early_in = sem("early_in")
        n1 = norm_sems(sem, "n1")
        qkv_filled = sem("l0_qkv_filled")
        ps = ctx.enter_context(nc.psum_tensor("psLane", [P, LANES, 1024], F32))

        def x_tile(t):
            return X[:, bass.ts(t, D)]

        phase_a(nc, a, X, mask, ident, neghalf, x_tile, ps, early, early_in, n1, qkv_filled)
        phase_rest(nc, a, X, mask, ident, neghalf, x_tile, ps, early, early_in, n1, qkv_filled)


def phase_a(nc, a, X, mask, ident, neghalf, x_tile, ps, early, early_in, n1, qkv_filled):
    ctx = ExitStack()
    with ctx:
        def sb(name, shape, dt=F32):
            return ctx.enter_context(nc.sbuf_tensor(name, shape, dt))

        def sem(name):
            return ctx.enter_context(nc.semaphore(name))

        WqT = sb("WqT", [P, DC, NKT * G * P])
        WkT = sb("WkT", [P, DC, KW])
        WvT = sb("WvT", [P, DC, KW])
        WoT = sb("WoT", [P, NKT * G, D])
        clast = sb("clast", [P, DC, B])
        hid = sb("hid", [P, TB, DC, S])
        xn = sb("xn", [P, D])
        xnT = sb("xnT", [P, DC, P])
        QT = sb("QT", [HD, KVH, TB, G * L])
        KT = sb("KT", [HD, 2, KVH, S])
        V = sb("V", [P, 2, 2, KW])
        Vlat = sb("Vlat", [P, KW])
        Vtail = sb("Vtail", [TAIL, TB, KW])
        probs = sb("probs", [P, KVH, S])
        probsT = sb("probsT", [P, 2, 3, P])
        O = sb("O", [P, KW])
        OT = sb("OT", [P, NKT, G, TB, L])
        work = sb("work", [P, DC, CTX])
        top = [sb(f"top{k}", [P, DC, 8]) for k in range(3)]
        top_last = sb("top_last", [P, DC, 8])
        gate = sb("gate", [P, 1])
        rmax = sb("rmax", [P, KVH])
        nmax = sb("nmax", [P, KVH])
        rsum = sb("rsum", [P, 2, KVH])
        rinv = sb("rinv", [P, KVH])
        stats = sb("stats", [P, 6])
        mv = sb("mv", [P, 2])
        veps = sb("veps", [P, 1])
        rstd = sb("rstd", [P, 1])
        starts_i = sb("starts_i", [NLR, 4], I32)
        starts = sb("starts", [NLR, 4])
        batches = sb("batches", [NLR, B])
        chosen = sb("chosen", [NLR, 1])
        reached = sb("reached", [NLR, B])
        taps = sb("taps", [P, 2 * TAPS])
        shifted = work[:].rearrange("p c n -> p (c n)")[:, 0:3 * P + TAPS - 1]
        vlast_dram = nc.dram_tensor("vlast_dram", [B, KW], F32, kind="Internal").ap()

        banks = ps[:].rearrange("p u (b n) -> p (u b) n", b=2)
        psKV, psS, psPT, psO, psM = banks[:, 0:2], banks[:, 2:4], banks[:, 4:6], banks[:, 6], banks[:, 7]
        small0 = {"stats": stats[:].unsqueeze(1), "mv": mv[:].unsqueeze(1), "veps": veps[:].unsqueeze(1),
                  "rstd": rstd[:].unsqueeze(1)}
        xn0 = xn[:].unsqueeze(1)

        const_in = sem("const_in")
        table_in = sem("table_in")
        adapter_step = sem("adapter_step")
        band_step = sem("band_step")
        x0_in = sem("x0_in")
        x_in = sem("x_in")
        wv_in = sem("wv_in")
        wq_in = sem("wq_in")
        wk_in = sem("wk_in")
        wo_in = sem("wo_in")
        ctx_in = [sem(f"ctx_in{j}") for j in range(TB)]
        zero_done = sem("zero_done")
        vlast_filled = sem("vlast_filled")
        vlast_evac = sem("vlast_evac")
        vlast_out = sem("vlast_out")
        vtail_in = sem("vtail_in")
        kv_filled = sem("kv_filled")
        kv_evac = sem("kv_evac")
        s_filled = sem("s_filled")
        rmax_done = sem("rmax_done")
        nmax_ready = sem("nmax_ready")
        exp_done = sem("exp_done")
        pt_filled = sem("pt_filled")
        pt_evac = sem("pt_evac")
        av_done = sem("av_done")
        recip_done = sem("recip_done")
        o_evac = sem("o_evac")
        m_filled = sem("m_filled")
        m_evac = sem("m_evac")
        topk_step = sem("topk_step")
        stats_done = sem("stats_done")
        veps_ready = sem("veps_ready")
        rstd_ready = sem("rstd_ready")
        xn_ready = sem("xn_ready")

        def kv(t, n):
            if isinstance(t, int) and t == 0 and n < 5:
                return 1 + n
            if isinstance(t, int) and t == -1 and n > 20:
                return 6 + n - 21
            return 4 + 24 * t + n

        def kv_bank(t, n):
            return (kv(t, n) if isinstance(t, int) else n) % 2

        def m_ot(t, j):
            return 6 * t + 1 + j if j < TB - 1 else 6 * (t + 1) - 1 - (1 if isinstance(t, int) and t == NT - 1 else 0)

        def m_proj(t):
            return m_ot(t, TB - 1) + 1

        def m_xt(t):
            return 6 * (t - 1) + 4 if not (isinstance(t, int) and t == 0) else 0

        def over_tiles(eng, body):
            body(0, True, False)
            with eng.Fori(1, NT - 1) as t:
                body(t, False, False)
            body(NT - 1, False, True)

        block = ctx.enter_context(nc.Block())

        @block.sync
        def _(sp):
            sp.dma_start(ident[:], a["ident"]).then_inc(const_in, 16)
            x_v = X[:].rearrange("p (t d) -> p t d", d=D)
            sp.dma_start(x_v[:, 0:1], a["x"][:, 0:1]).then_inc(x0_in, 16)
            sp.dma_start(clast[:], a["ctx_last"]).then_inc(const_in, 16)
            sp.dma_start(WvT[:], a["WvT"]).then_inc(wv_in, 16)
            sp.dma_start(WkT[:], a["WkT"]).then_inc(wk_in, 16)
            sp.dma_start(hid[:, 0, :, 0:CTX], a["ctxT"][0]).then_inc(ctx_in[0], 16)
            for c in range(DC):
                sp.dma_start(WqT[:, c], a["WqT"][:, c]).then_inc(wq_in, 16)
            for j in range(1, TB):
                sp.dma_start(hid[:, j, :, 0:CTX], a["ctxT"][j]).then_inc(ctx_in[j], 16)
            sp.dma_start(shifted, a["shifted"]).then_inc(table_in, 16)
            sp.dma_start(taps[:], a["taps"].rearrange("(o n) -> o n", o=1).to_broadcast([P, 2 * TAPS])).then_inc(table_in, 16)
            sp.dma_start(batches[:], a["batches"]).then_inc(table_in, 16)
            sp.dma_start(chosen[:], a["chosen"]).then_inc(table_in, 16)
            sp.dma_start(starts_i[:], a["starts"].rearrange("(o n) -> o n", o=1).to_broadcast([NLR, 4])).then_inc(table_in, 16)
            sp.dma_start(x_v[:, 1:NT], a["x"][:, 1:NT]).then_inc(x_in, 16)
            sp.dma_start(WoT[:], a["WoT"]).then_inc(wo_in, 16)
            sp.wait_ge(vlast_evac, 1)
            sp.dma_start(vlast_dram, O[0:B, :]).then_inc(vlast_out, 16)
            sp.wait_ge(vlast_out, 16)

            def load_tail(t):
                wait(sp, av_done, 16 * t)
                sp.dma_start(Vtail[0:1, :, :].rearrange("a j n -> a (j n)"),
                             vlast_dram[bass.ts(t, TB), :].rearrange("(a j) n -> a (j n)", a=1)).then_inc(vtail_in, 16)
                wait(sp, kv_evac, kv(t - 1, 20) + 1)
                for j in range(TB):
                    sp.dma_start(Vtail[1:TAIL, j, :], Vlat[L * j:L * j + L, :]).then_inc(vtail_in, 16)

            load_tail(0)

            def body(t, first, last):
                if last:
                    for k, name in (("w_qkv", "w_qkv0"), ("w_o", "w_o0"), ("w_ffn", "w_ffn0"), ("loraA", "loraA"),
                                    ("cos", "cos"), ("sin", "sin"), ("causal", "causal"), ("block16", "block16"),
                                    ("jmask", "jmask")):
                        sp.dma_start(early[k][:], a[name]).then_inc(early_in, 16)
                    return
                for j in range(TB):
                    sp.wait_ge(kv_filled, kv(t, 5 * j + 4) + 1)
                    sp.wait_ge(topk_step, 8 * (TB * t + j) + 2)
                    sp.dma_start(hid[:, j, :, 0:CTX], a["ctxT"][TB * (t + 1) + j]).then_inc(ctx_in[j], 16)
                load_tail(t + 1)

            over_tiles(sp, body)

        @block.gpsimd
        def _(pool):
            pool.memset(neghalf[:], -0.5).then_inc(zero_done, 1)
            pool.memset(top_last[:], GONE).then_inc(zero_done, 1)
            pool.wait_ge(zero_done, 2)

            def rstd_of(t):
                wait(pool, xn_ready, t)
                pool.wait_ge(veps_ready, t + 1)
                pool.tensor_tensor(rstd[:], veps[:], neghalf[:], ALU.pow).then_inc(rstd_ready, 1)

            rstd_of(0)
            with pool.Fori(1, NT) as t:
                rstd_of(t)
            pool.wait_ge(xn_ready, NT)
            norm_rstd(pool, n1, 0, 0, small0, neghalf)

        @block.tensor
        def _(pe):
            def next_bank(t, n):
                wait(pe, kv_evac, kv(t, n) - 1)
                return psKV[:, kv_bank(t, n), :]

            def xt(t):
                pe.wait_ge(xn_ready, t + 1)
                wait(pe, m_evac, m_xt(t))
                for c in range(DC):
                    mm = pe.transpose(psM[:, P * c:P * c + P], xn[:, P * c:P * c + P], ident[:])
                mm.then_inc(m_filled, 1)

            def v_latents(t):
                out = next_bank(t - 1, 20)
                pe.wait_ge(m_evac, m_xt(t) + 1)
                for c in range(DC):
                    mm = pe.matmul(out[:, 0:KW], xnT[:, c, :], WvT[:, c, :], start=(c == 0), stop=(c == DC - 1))
                mm.then_inc(kv_filled, 1)

            def q(t, k):
                out = next_bank(t - 1, 21 + k)
                for r in range(G):
                    for c in range(DC):
                        w = P * (G * k + r)
                        mm = pe.matmul(out[:, P * r:P * r + P], WqT[:, c, w:w + P], xnT[:, c, :],
                                       start=(c == 0), stop=(c == DC - 1))
                mm.then_inc(kv_filled, 1)

            def k_part(t, j, k):
                out = next_bank(t, 5 * j + k)
                if k == 0:
                    pe.wait_ge(ctx_in[j], 16 * (t + 1))
                    pe.wait_ge(m_evac, m_xt(t) + 1)
                for c in range(DC):
                    mm = pe.matmul(out[:, 0:S], WkT[:, c, P * k:P * k + P], hid[:, j, c, :],
                                   start=(c == 0), stop=(c == DC - 1))
                mm.then_inc(kv_filled, 1)

            def v_part(t, j, s):
                out = next_bank(t, 5 * j + 3 + s)
                for c in range(DC):
                    mm = pe.matmul(out[:, 0:KW], hid[:, j, c, P * s:P * s + P], WvT[:, c, :],
                                   start=(c == 0), stop=(c == DC - 1))
                mm.then_inc(kv_filled, 1)

            def scores(t, j, h):
                b = TB * t + j
                wait(pe, exp_done, 4 * b + 2 * h)
                if h == 0:
                    pe.wait_ge(kv_evac, kv(t, 5 * j + 2) + 1)
                for g in (2 * h, 2 * h + 1):
                    mm = pe.matmul(psS[:, g % 2, 0:S], QT[:, g, j, :], KT[:, j % 2, g, :], start=True, stop=True)
                mm.then_inc(s_filled, 1)

            def turn_probs(t, j, g):
                at = 4 * (TB * t + j) + g
                pe.wait_ge(exp_done, at + 1)
                wait(pe, pt_evac, at - 1)
                for k, (lo, hi) in enumerate(((0, P), (P, 2 * P), (2 * P, S))):
                    mm = pe.transpose(psPT[0:hi - lo, g % 2, P * k:P * k + P], probs[:, g, lo:hi], ident[:])
                mm.then_inc(pt_filled, 1)

            def values(t, j, g):
                b = TB * t + j
                pe.wait_ge(pt_evac, 4 * b + g + 1)
                if g == 0:
                    pe.wait_ge(kv_evac, kv(t, 5 * j + 4) + 1)
                    pe.wait_ge(vtail_in, 80 * (t + 1))
                    wait(pe, o_evac, b)
                out = psO[:, HD * g:HD * g + HD]
                cols = slice(HD * g, HD * g + HD)
                pe.matmul(out, probsT[:, g % 2, 0, :], V[:, j % 2, 0, cols], start=True, stop=False)
                pe.matmul(out, probsT[:, g % 2, 1, :], V[:, j % 2, 1, cols], start=False, stop=False)
                pe.matmul(out, probsT[0:TAIL, g % 2, 2, :], Vtail[:, j, cols],
                          start=False, stop=True).then_inc(av_done, 1)

            def next_turn():
                pe.wait_ge(m_evac, m_ot(NT - 1, TB - 2) + 1)
                norm_turn(pe, n1, 0, 0, xn0, psM, ident)

            def next_qkv():
                pe.wait_ge(kv_evac, kv(NT - 1, 19) + 1)
                pe.wait_ge(n1["xnT"], 1)
                pe.wait_ge(early_in, 16 * EARLY_LOADS)
                self_qkv(pe, psKV[:, 0], psKV[:, 1], xnT, early["w_qkv"]).then_inc(qkv_filled, 1)

            def turn_out(t, j):
                if isinstance(t, int) and (t, j) == (NT - 1, TB - 1):
                    pe.wait_ge(n1["xnT"], 1)
                pe.wait_ge(m_evac, m_ot(t, j))
                pe.wait_ge(o_evac, TB * t + j + 1)
                for k in range(NKT):
                    mm = pe.transpose(psM[:, P * k:P * k + P], O[:, P * k:P * k + P], ident[:])
                mm.then_inc(m_filled, 1)

            def project(t):
                pe.wait_ge(m_evac, m_proj(t))
                for n in range(NKT * G):
                    mm = pe.matmul(psM, OT[:, n // G, n % G].rearrange("p j q -> p (j q)"), WoT[:, n, :],
                                   start=(n == 0), stop=(n == NKT * G - 1))
                mm.then_inc(m_filled, 1)

            pe.wait_ge(const_in, 32)
            pe.wait_ge(wv_in, 16)
            for c in range(DC):
                mm = pe.matmul(psS[0:B, 0, 0:KW], clast[:, c, :], WvT[:, c, :], start=(c == 0), stop=(c == DC - 1))
            mm.then_inc(vlast_filled, 1)
            xt(0)
            v_latents(0)
            pe.wait_ge(wk_in, 16)
            pe.wait_ge(vlast_evac, 1)

            def body(t, first, last):
                k_part(t, 0, 0)
                k_part(t, 0, 1)
                if not first:
                    turn_out(t - 1, TB - 1)
                k_part(t, 0, 2)
                v_part(t, 0, 0)
                v_part(t, 0, 1)
                if first:
                    pe.wait_ge(wq_in, 64)
                    for k in range(NKT):
                        q(0, k)
                    pe.wait_ge(kv_evac, kv(-1, 23) + 1)
                else:
                    project(t - 1)
                for j in range(TB):
                    scores(t, j, 0)
                    if j < TB - 1:
                        k_part(t, j + 1, 0)
                        if j:
                            turn_out(t, j - 1)
                        k_part(t, j + 1, 1)
                    else:
                        v_part(t, j, 1)
                        turn_out(t, j - 1)
                    turn_probs(t, j, 0)
                    turn_probs(t, j, 1)
                    if j == TB - 1:
                        next_turn() if last else xt(t + 1)
                    scores(t, j, 1)
                    values(t, j, 0)
                    if j < TB - 1:
                        k_part(t, j + 1, 2)
                        values(t, j, 1)
                        if j < TB - 2:
                            v_part(t, j + 1, 0)
                            turn_probs(t, j, 2)
                            turn_probs(t, j, 3)
                            v_part(t, j + 1, 1)
                        else:
                            turn_probs(t, j, 2)
                            turn_probs(t, j, 3)
                            v_part(t, j + 1, 0)
                    else:
                        if not last:
                            v_latents(t + 1)
                        values(t, j, 1)
                        if not last:
                            q(t + 1, 0)
                        turn_probs(t, j, 2)
                        turn_probs(t, j, 3)
                        if last:
                            next_qkv()
                        else:
                            q(t + 1, 1)
                            q(t + 1, 2)
                    values(t, j, 2)
                    values(t, j, 3)
                if first:
                    pe.wait_ge(wo_in, 16)

            over_tiles(pe, body)
            turn_out(NT - 1, TB - 1)
            project(NT - 1)

        @block.scalar
        def _(act):
            def evac_k(t, j, k):
                act.wait_ge(kv_filled, kv(t, 5 * j + k) + 1)
                if k == 0:
                    wait(act, s_filled, 2 * (TB * t + j) - 2)
                for g, tile, lo, hi, at in PARTS:
                    if tile == k:
                        ins = act.activation(KT[at:at + hi - lo, j % 2, g, :], psKV[lo:hi, kv_bank(t, 5 * j + k), 0:S],
                                             ACT.Copy)
                ins.then_inc(kv_evac, 1)

            def evac_v(t, j, s):
                act.wait_ge(kv_filled, kv(t, 5 * j + 3 + s) + 1)
                if s == 0:
                    wait(act, av_done, 4 * (TB * t + j) - 4)
                act.activation(V[:, j % 2, s, :], psKV[:, kv_bank(t, 5 * j + 3 + s), 0:KW], ACT.Copy).then_inc(kv_evac, 1)

            def evac_v_latents(t):
                wait(act, vtail_in, 80 * t)
                act.wait_ge(kv_filled, kv(t - 1, 20) + 1)
                act.activation(Vlat[:], psKV[:, kv_bank(t - 1, 20), 0:KW], ACT.Copy).then_inc(kv_evac, 1)

            def evac_q(t, k):
                wait(act, s_filled, 2 * TB * t)
                act.wait_ge(kv_filled, kv(t - 1, 21 + k) + 1)
                src = psKV[:, kv_bank(t - 1, 21 + k), :].rearrange("p (r j q) -> p r j q", r=G, j=TB)
                for g, tile, lo, hi, at in PARTS:
                    if tile == k:
                        ins = act.activation(QT[at:at + hi - lo, g].rearrange("p j (r q) -> p r j q", r=G), src[lo:hi],
                                             ACT.Copy)
                ins.then_inc(kv_evac, 1)

            def exps(t, j, h):
                b = TB * t + j
                act.wait_ge(nmax_ready, 2 * b + h + 1)
                wait(act, pt_filled, 4 * b + 2 * h - 2)
                if h == 0:
                    wait(act, recip_done, b - 1)
                for g in (2 * h, 2 * h + 1):
                    act.activation(probs[:, g, :], psS[:, g % 2, 0:S], ACT.Exp, bias=nmax[:, g:g + 1],
                                   scale=XSCALE, accum_out=rsum[:, j % 2, g:g + 1]).then_inc(exp_done, 1)

            def evac_probs(t, j, g):
                at = 4 * (TB * t + j) + g
                act.wait_ge(pt_filled, at + 1)
                wait(act, av_done, at - 1)
                act.activation(probsT[:, g % 2, 0:2, :].rearrange("p a q -> p (a q)"), psPT[:, g % 2, 0:2 * P], ACT.Copy)
                act.activation(probsT[0:TAIL, g % 2, 2, :], psPT[0:TAIL, g % 2, 2 * P:3 * P],
                               ACT.Copy).then_inc(pt_evac, 1)

            act.wait_ge(vlast_filled, 1)
            act.activation(O[0:B, :], psS[0:B, 0, 0:KW], ACT.Copy).then_inc(vlast_evac, 1)
            evac_v_latents(0)

            def body(t, first, last):
                for k in range(NKT):
                    evac_k(t, 0, k)
                evac_v(t, 0, 0)
                evac_v(t, 0, 1)
                if first:
                    for k in range(NKT):
                        evac_q(0, k)
                for j in range(TB):
                    exps(t, j, 0)
                    if j < TB - 1:
                        evac_k(t, j + 1, 0)
                        evac_k(t, j + 1, 1)
                    else:
                        evac_v(t, j, 1)
                    evac_probs(t, j, 0)
                    evac_probs(t, j, 1)
                    if last and j == TB - 1:
                        act.wait_ge(n1["xt"], 1)
                        act.activation(xnT[:].rearrange("p c q -> p (c q)"), psM, ACT.Copy).then_inc(n1["xnT"], 1)
                    exps(t, j, 1)
                    if j < TB - 2:
                        evac_k(t, j + 1, 2)
                        evac_v(t, j + 1, 0)
                        evac_probs(t, j, 2)
                        evac_probs(t, j, 3)
                        evac_v(t, j + 1, 1)
                    elif j == TB - 2:
                        evac_k(t, j + 1, 2)
                        evac_probs(t, j, 2)
                        evac_probs(t, j, 3)
                        evac_v(t, j + 1, 0)
                    else:
                        if not last:
                            evac_v_latents(t + 1)
                            evac_q(t + 1, 0)
                        evac_probs(t, j, 2)
                        evac_probs(t, j, 3)
                        if not last:
                            evac_q(t + 1, 1)
                            evac_q(t + 1, 2)

            over_tiles(act, body)

        @block.vector
        def _(dve):
            def norm_stats(t):
                wait(dve, xn_ready, t)
                dve.bn_stats(stats[:], x_tile(t)).then_inc(stats_done, 1)
                dve.wait_ge(stats_done, 2 * t + 1)
                wait(dve, rstd_ready, t)
                dve.memset(gate[:], 0.0)
                dve.bn_aggr(mv[:], stats[:]).then_inc(stats_done, 1)
                dve.wait_ge(stats_done, 2 * t + 2)
                dve.tensor_scalar(veps[:], mv[:, 1:2], EPS, None, ALU.add).then_inc(veps_ready, 1)

            def norm(t):
                dve.wait_ge(rstd_ready, t + 1)
                wait(dve, m_filled, m_xt(t - 1) + 1 if not (isinstance(t, int) and t == 0) else 0)
                dve.tensor_scalar(xn[:], x_tile(t), mv[:, 0:1], rstd[:, 0:1], ALU.subtract, ALU.mult)\
                   .then_inc(xn_ready, 1)

            def next_stats():
                def before():
                    dve.wait_ge(xn_ready, NT)
                    dve.wait_ge(topk_step, 8 * (TB * (NT - 1) + 1) + 2)
                tile_stats(dve, n1, 0, 0, x_tile(0), small0, gate, before)

            def next_rows():
                dve.wait_ge(m_filled, m_xt(NT - 1) + 1)
                norm_rows(dve, n1, 0, 0, x_tile(0), small0, xn0)

            def evac_xt(t):
                wait(dve, kv_filled, kv(t - 1, 20))
                dve.wait_ge(m_filled, m_xt(t) + 1)
                dve.tensor_copy(xnT[:].rearrange("p c q -> p (c q)"), psM)
                dve.tensor_copy(hid[:, :, :, CTX:S], psM.rearrange("p (c j q) -> p j c q", c=DC, j=TB))\
                   .then_inc(m_evac, 1)

            def row_max(t, j, h):
                b = TB * t + j
                dve.wait_ge(s_filled, 2 * b + h + 1)
                wait(dve, nmax_ready, 2 * b + h)
                dve.tensor_reduce(rmax[:, 2 * h:2 * h + 2], psS[:, :, 0:S], AX.X, ALU.max).then_inc(rmax_done, 1)
                dve.wait_ge(rmax_done, 2 * b + h + 1)
                wait(dve, exp_done, 4 * b + 2 * h - 2)
                dve.tensor_scalar(nmax[:, 2 * h:2 * h + 2], rmax[:, 2 * h:2 * h + 2], -XSCALE, None, ALU.mult)\
                   .then_inc(nmax_ready, 1)

            def evac_out(t, j):
                b = TB * t + j
                dve.wait_ge(exp_done, 4 * b + 4)
                wait(dve, o_evac, b)
                dve.reciprocal(rinv[:], rsum[:, j % 2, :]).then_inc(recip_done, 1)
                dve.wait_ge(recip_done, b + 1)
                dve.wait_ge(av_done, 4 * b + 4)
                wait(dve, m_filled, m_ot(t, j) if j else m_ot(t, 0) - 1)
                dve.tensor_tensor(O[:].rearrange("p (g d) -> p g d", g=KVH),
                                  psO[:, 0:KW].rearrange("p (g d) -> p g d", g=KVH),
                                  rinv[:].unsqueeze(2).to_broadcast([P, KVH, HD]), ALU.mult).then_inc(o_evac, 1)

            def evac_ot(t, j):
                dve.wait_ge(m_filled, m_ot(t, j) + 1)
                dve.tensor_copy(OT[:, :, :, j, :], psM[:, 0:KW].rearrange("p (k r q) -> p k r q", k=NKT, r=G))\
                   .then_inc(m_evac, 1)

            def add_projected(t):
                dve.wait_ge(m_filled, m_proj(t) + 1)
                dve.tensor_tensor(x_tile(t), x_tile(t), psM[:], ALU.add).then_inc(m_evac, 1)

            def topk(t, j, step):
                b = TB * t + j
                if step in (1, 2, 3, 4, 5, 7):
                    wait(dve, topk_step, 8 * b + step - 1)
                    if step == 1:
                        dve.wait_ge(ctx_in[j], 16 * (t + 1))
                    dve.memset(gate[:], 0.0)
                src = hid[:, j, :, 0:CTX]
                if step in (1, 3, 5):
                    for c in range(DC):
                        ins = dve.max(top[step // 2][:, c, :], src[:, c, :] if step == 1 else work[:, c, :])
                elif step in (2, 4, 7):
                    picked = {2: top[0], 4: top[1], 7: top_last}[step]
                    for c in range(DC):
                        ins = dve.match_replace(work[:, c, :], picked[:, c, :],
                                                src[:, c, :] if step == 2 else work[:, c, :], GONE)
                elif step == 6:
                    dve.wait_ge(topk_step, 8 * b + 5)
                    ins = dve.tensor_copy(top_last[:, :, 0:4], top[2][:, :, 0:4])
                else:
                    dve.wait_ge(topk_step, 8 * b + 7)
                    ins = dve.tensor_scalar(mask[:, :, bass.ts(b, L)], work[:, :, 0:L], GONE, None, ALU.is_le)
                ins.then_inc(topk_step, 1)

            def choose_adapters():
                adapter = early["adapter"]
                dve.tensor_copy(starts[:], starts_i[:]).then_inc(adapter_step, 1)
                dve.wait_ge(adapter_step, 1)
                dve.tensor_scalar(reached[:], batches[:], starts[:, 0:1], None, ALU.is_ge).then_inc(adapter_step, 1)
                for k in range(1, 4):
                    dve.wait_ge(adapter_step, k + 1)
                    dve.scalar_tensor_tensor(out=reached[:], in0=batches[:], scalar=starts[:, k:k + 1], in1=reached[:],
                                             op0=ALU.is_ge, op1=ALU.add).then_inc(adapter_step, 1)
                dve.wait_ge(adapter_step, 5)
                dve.tensor_scalar(adapter[:], reached[:], chosen[:, 0:1], None, ALU.is_equal).then_inc(adapter_step, 1)

            def build_bands():
                band = early["band"]
                for tap in range(TAPS):
                    for ch in range(2):
                        w = taps[:, TAPS * ch + tap:TAPS * ch + tap + 1]
                        src = shifted[:, tap:tap + 3 * P]
                        if tap == 0:
                            ins = dve.tensor_scalar(band[:, ch], src, w, None, ALU.mult)
                        else:
                            dve.wait_ge(band_step, 2 * (tap - 1) + ch + 1)
                            ins = dve.scalar_tensor_tensor(out=band[:, ch], in0=src, scalar=w, in1=band[:, ch],
                                                           op0=ALU.mult, op1=ALU.add)
                        ins.then_inc(band_step, 1)
                dve.wait_ge(band_step, 2 * TAPS)

            dve.wait_ge(x0_in, 16)
            norm_stats(0)
            norm(0)
            evac_xt(0)
            dve.wait_ge(table_in, 80)
            choose_adapters()
            build_bands()
            dve.wait_ge(zero_done, 2)
            dve.wait_ge(x_in, 16)
            dve.wait_ge(vlast_out, 16)

            def body(t, first, last):
                if not first:
                    evac_out(t - 1, TB - 1)
                    evac_ot(t - 1, TB - 1)
                    add_projected(t - 1)
                for j in range(TB):
                    if j:
                        evac_out(t, j - 1)
                    row_max(t, j, 0)
                    topk(t, j, 1)
                    if j:
                        evac_ot(t, j - 1)
                    if j == TB - 1 and not last:
                        evac_xt(t + 1)
                    topk(t, j, 2)
                    if j == 1:
                        next_stats() if last else norm_stats(t + 1)
                    if j == 2:
                        next_rows() if last else norm(t + 1)
                    row_max(t, j, 1)
                    if j == TB - 1 and last:
                        topk(t, j, 3)
                        evac_out(t, j)
                        topk(t, j, 4)
                        evac_ot(t, j)
                    for step in range(5 if j == TB - 1 and last else 3, 9):
                        topk(t, j, step)

            over_tiles(dve, body)
            add_projected(NT - 1)


def phase_rest(nc, a, X, mask, ident, neghalf, x_tile, ps, early, early_in, n1, qkv_filled):
    ctx = ExitStack()
    with ctx:
        def sb(name, shape, dt=F32):
            return ctx.enter_context(nc.sbuf_tensor(name, shape, dt))

        posT = sb("posT", [P, DC, NT * P])
        Y = sb("Y", [P, DC, 2, 2, B])
        lanes = sb("lanes", [P, LANES, 2, 1024])
        xn = sb("lane_xn", [P, LANES, D])
        xnT = sb("lane_xnT", [P, LANES, DC, P])
        small = {k: sb(f"lane_{k}", [P, LANES, n]) for k, n in
                 (("stats", 6), ("mv", 2), ("veps", 1), ("rstd", 1), ("rmax", 32), ("rinv", 32), ("rsum", 8))}
        ones = sb("ones", [P, P])
        bufs = (posT, Y, lanes, xn, xnT, small, early["jmask"], ones)
        blend = sb("blend", [P, DC, 2, B])
        affine = sb("affine", [P, 2])
        late = {k: sb(f"{k}1", shape, dt) for k, shape, dt in (
            ("w_o", [P, EW // P, D], F32), ("w_ffn", [P, DC, D], F32),
            ("ffn_mask", [P, DC, D], U8), ("b_qk", [P, 4], F32), ("b_v", [P, EW], F32), ("b_o", [P, D], F32),
            ("keep", [P, 2, L], F32))}
        late["w_qkv"] = early["w_qkv"]
        late_in = ctx.enter_context(nc.semaphore("late_in"))

        layer0(nc, a, X, mask, ident, neghalf, x_tile, ps, bufs, early, n1, qkv_filled, affine, late, late_in)
        mix_gates(nc, neghalf, ps, Y, ones, blend, early["band"], affine, late, late_in)
        layer1(nc, a, X, mask, ident, neghalf, x_tile, ps, bufs, blend, late)


def norm_sems(sem, name):
    return {k: sem(f"{name}_{k}") for k in ("stats", "aggr", "veps", "rstd", "xn", "xt", "xnT")}


def tile_stats(dve, n, t, u, x, small, gate, before):
    before()
    dve.memset(gate[:], 0.0)
    dve.bn_stats(small["stats"][:, u], x).then_inc(n["stats"], 1)
    dve.wait_ge(n["stats"], t + 1)
    dve.memset(gate[:], 0.0)
    dve.bn_aggr(small["mv"][:, u], small["stats"][:, u]).then_inc(n["aggr"], 1)
    dve.wait_ge(n["aggr"], t + 1)
    dve.tensor_scalar(small["veps"][:, u], small["mv"][:, u, 1:2], EPS, None, ALU.add).then_inc(n["veps"], 1)


def norm_rstd(pool, n, t, u, small, neghalf):
    pool.wait_ge(n["veps"], t + 1)
    pool.tensor_tensor(small["rstd"][:, u], small["veps"][:, u], neghalf[:], ALU.pow).then_inc(n["rstd"], 1)


def norm_rows(dve, n, t, u, x, small, xn):
    dve.wait_ge(n["rstd"], t + 1)
    dve.tensor_scalar(xn[:, u], x, small["mv"][:, u, 0:1], small["rstd"][:, u, 0:1],
                      ALU.subtract, ALU.mult).then_inc(n["xn"], 1)


def self_qkv(pe, low, high, xnT, w_qkv):
    for c in range(DC):
        pe.matmul(low, xnT[:, c], w_qkv[:, c, 0:AQ], start=(c == 0), stop=(c == DC - 1))
    for c in range(DC):
        mm = pe.matmul(high[:, 0:2 * AKV], xnT[:, c], w_qkv[:, c, AQ:], start=(c == 0), stop=(c == DC - 1))
    return mm


def norm_turn(pe, n, t, u, xn, out, ident):
    pe.wait_ge(n["xn"], t + 1)
    for c in range(DC):
        mm = pe.transpose(out[:, P * c:P * c + P], xn[:, u, P * c:P * c + P], ident[:])
    mm.then_inc(n["xt"], 1)


SLOTS0 = {
    "stats1": 0.009, "rstd1": 0.009, "rows1": 0.017, "turn1": 0.135, "xnT1": 0.267, "qkv": 0.424, "rope": 0.811,
    "spread_v": 0.811, "rope_sum": 0.811, "turn_qk": 0.942, "evac_q": 0.984, "spread_k": 0.976, "scores": 1.101,
    "mask": 1.101, "shift": 1.191, "exps": 1.549, "turn_probs": 1.640, "evac_pt": 1.674, "values": 1.867,
    "normalise": 1.910, "turn_out": 2.041, "evac_ot": 2.041, "project": 2.134, "add_proj": 2.135,
    "stats2": 2.150, "rstd2": 2.283, "rows2": 2.330, "turn2": 2.532, "xnT2": 2.592, "lora_down": 2.680,
    "lora_mask": 2.841, "ffn": 2.960, "lora_up": 3.145, "add_ffn": 3.185, "stats3": 3.267, "rstd3": 3.331,
    "rows3": 3.372, "turn3": 3.726, "pos": 3.726, "crucial": 3.845, "rest": 3.909, "reduce_crucial": 3.968,
    "reduce_rest": 3.994,}
SLOTS1 = {
    "gate": 0.000, "add_rest": 0.027, "mix": 0.173, "turn_mix": 0.485, "add_mix": 0.614, "stats1": 0.707,
    "rstd1": 0.773, "rows1": 0.929, "bias": 2.451, "turn1": 0.989, "xnT1": 1.045, "qkv": 1.310,
    "evac_qk": 1.590, "evac_v": 1.762, "spread_k": 1.808, "scores": 2.006, "mask": 2.056, "shift": 2.136,
    "exps": 2.342, "spread_p": 2.461, "turn_probs": 2.571, "evac_pt": 2.710, "values": 2.919, "evac_ot": 2.919,
    "project": 3.015, "add_proj": 3.074, "stats2": 3.162, "rstd2": 3.245, "rows2": 3.395, "turn2": 3.500,
    "xnT2": 3.539, "ffn": 3.877, "add_ffn": 3.989, "store": 3.989,}
STARTS0 = ((0.00, 0.95, 1.89, 2.83, 3.83, 4.85, 5.82, 6.78),
           (0.00, 125.42, 126.89, 127.46))
STARTS1 = ((0.00, 0.45, 0.99, 1.56, 3.50, 4.58, 5.35, 6.53),
           (0.00, 37.47, 38.83, 39.38))


def over_lanes(eng, slots, starts, stages):
    run = list(stages.values())
    slot = [slots[name] for name in stages]
    order = sorted((k + x, k, n) for n, x in enumerate(slot) for k in range(1 - LANES, LANES) if 0 <= k + x < LANES)
    opening, closing = starts
    first = sorted((opening[t] + x, t, n) for n, x in enumerate(slot) for t in range(2 * LANES) if t + x < 2 * LANES)
    last = sorted((closing[t + LANES - NT] + x, t, n) for n, x in enumerate(slot) for t in range(NT - LANES, NT)
                  if t + x >= NT)
    for _, t, n in first:
        run[n](t, t % LANES)
    with eng.Fori(2, NT // LANES) as i:
        for _, k, n in order:
            run[n](LANES * i + k, k % LANES)
    for _, t, n in last:
        run[n](t, t % LANES)


def layer0(nc, a, X, mask, ident, neghalf, x_tile, ps, bufs, early, n1, qkv_filled, affine, late, late_in):
    posT, Y, lanes, xn, xnT, small, jmask, ones = bufs
    ctx = ExitStack()
    with ctx:
        def sb(name, shape, dt=F32):
            return ctx.enter_context(nc.sbuf_tensor(name, shape, dt))

        def sem(name):
            return ctx.enter_context(nc.semaphore(name))

        w_qkv, w_o, w_ffn, loraA, cos, sin, causal, block16, adapter = (
            early[k] for k in ("w_qkv", "w_o", "w_ffn", "loraA", "cos", "sin", "causal", "block16", "adapter"))
        loraB = sb("loraB", [BIAS_ROW + 1, D])
        lora_t = sb("lora_t", [BIAS_ROW + 1, LANES, P])
        QT = sb("lane_QT", [P, LANES, TB, P])
        Vd = sb("lane_Vd", [P, LANES, AKVH, TB, AD + 1])
        gate = sb("gate0", [P, 1])

        w_in = sem("l0_w_in")
        zero_done = sem("l0_zero_done")
        ones_done = sem("l0_ones_done")
        n2, n3 = norm_sems(sem, "n2"), norm_sems(sem, "n3")
        names = ("cos_done", "rope_terms", "roped", "v_spread", "qk_turned", "qt_ready", "kd_ready",
                 "s_filled", "s_masked", "max_done", "s_shifted", "p_ready", "pt_filled", "pt_ready", "av_filled",
                 "rinv_ready", "o_ready", "ot_filled", "ot_ready", "proj_filled", "proj_added", "lora_filled",
                 "lora_ready", "ffn_filled", "ffn_added", "crucial_ready", "rest_ready", "crucial_reduced",
                 "rest_reduced")
        s = {k: sem(f"l0_{k}") for k in names}
        s["qkv_filled"] = qkv_filled

        def after_first(stage):
            return lambda t, u: None if isinstance(t, int) and t == 0 else stage(t, u)

        terms = lambda u: lanes[:, u, 0, 0:QKH * AD]
        roped = lambda u: lanes[:, u, 1, 0:QKH * AD]
        Kd = lambda u: lanes[:, u, 0, 0:4 * P].rearrange("p (j g k) -> p j g k", j=TB, g=4)
        sm = lambda u: lanes[:, u, 0]
        probs = lambda u: lanes[:, u, 1]
        pT = lambda u: lanes[:, u, 0]
        O = lambda u: xn[:, u]
        OT = lambda u: xnT[:, u]
        crucial = lambda u: lanes[:, u, 0, 0:D]
        rest = lambda u: lanes[:, u, 0, D:2 * D]
        low = lambda u: ps[:, u, 0:512]
        high = lambda u: ps[:, u, 512:1024]

        block = ctx.enter_context(nc.Block())

        @block.sync
        def _(sp):
            row = lambda x, n: x.rearrange("(o n) -> o n", o=1).to_broadcast([P, n])
            sp.dma_start(loraB[BIAS_ROW:BIAS_ROW + 1, :], a["ffn_bias"].rearrange("(o n) -> o n", o=1)).then_inc(w_in, 16)
            sp.wait_ge(zero_done, 3)
            sp.dma_start(loraB[0:NLR, :], a["loraB"]).then_inc(w_in, 16)
            for dst, src in ((affine[:, 0:1], row(a["bn_gamma"], 1)), (affine[:, 1:2], row(a["bn_beta"], 1)),
                             (late["w_ffn"][:], a["w_ffn1"]), (late["ffn_mask"][:], a["ffn_mask"]),
                             (late["w_o"][:], a["w_o1"]), (late["b_qk"][:], a["b_qk1"]),
                             (late["b_v"][:], row(a["b_v1"], EW)), (late["b_o"][:], row(a["b_o1"], D)),
                             (late["keep"][:, 0], a["keep1"]), (late["keep"][:, 1], a["masked1"])):
                sp.dma_start(dst, src).then_inc(late_in, 16)
            sp.wait_ge(s["qkv_filled"], NT)
            sp.dma_start(late["w_qkv"][:], a["w_qkv1"]).then_inc(late_in, 16)

        @block.gpsimd
        def _(pool):
            def clear_v(part, us):
                pool.memset(Vd[:, us], 0.0).then_inc(zero_done, 1)
                pool.wait_ge(zero_done, 1 + part)
                for j in range(TB):
                    wait(pool, ones_done, TB * part + j)
                    pool.memset(Vd[L * j:L * j + L, us, :, j, AD:AD + 1], 1.0).then_inc(ones_done, 1)
                pool.wait_ge(ones_done, TB * (part + 1))

            def clear_rest():
                clear_v(1, slice(1, LANES))
                pool.memset(loraB[0:BIAS_ROW, :], 0.0).then_inc(zero_done, 1)
                pool.wait_ge(zero_done, 3)
                pool.memset(lora_t[0:BIAS_ROW], 0.0).then_inc(zero_done, 1)
                pool.wait_ge(zero_done, 4)
                pool.memset(lora_t[BIAS_ROW:BIAS_ROW + 1], 1.0).then_inc(zero_done, 1)
                pool.wait_ge(zero_done, 5)
                pool.memset(ones[:], 1.0).then_inc(ones_done, 1)
                pool.wait_ge(ones_done, 1 + 2 * TB)

            def first_rstd(t, u):
                norm_rstd(pool, n1, t, u, small, neghalf)
                if isinstance(t, int) and t == 1:
                    clear_rest()

            clear_v(0, slice(0, 1))

            def rope_sum(t, u):
                pool.wait_ge(s["rope_terms"], t + 1)
                pool.tensor_tensor(roped(u), roped(u), terms(u), ALU.add).then_inc(s["roped"], 1)

            def shift(t, u):
                pool.wait_ge(s["max_done"], t + 1)
                v = sm(u).rearrange("p (n k) -> p n k", k=L)
                pool.tensor_tensor(v, v, small["rmax"][:, u].unsqueeze(2).to_broadcast([P, 32, L]), ALU.subtract)\
                    .then_inc(s["s_shifted"], 1)

            def rest_features(t, u):
                pool.wait_ge(s["crucial_ready"], t + 1)
                pool.tensor_tensor(rest(u).rearrange("p (c n) -> p c n", c=DC), posT[:, :, bass.ts(t, P)],
                                   crucial(u).rearrange("p (c n) -> p c n", c=DC), ALU.subtract)\
                    .then_inc(s["rest_ready"], 1)

            over_lanes(pool, SLOTS0, STARTS0, {
                "rstd1": after_first(first_rstd),
                "rope_sum": rope_sum, "shift": shift,
                "rstd2": lambda t, u: norm_rstd(pool, n2, t, u, small, neghalf),
                "rstd3": lambda t, u: norm_rstd(pool, n3, t, u, small, neghalf), "rest": rest_features})

        @block.tensor
        def _(pe):
            def first_turn(t, u):
                wait(pe, n3["xnT"], t - LANES + 1)
                norm_turn(pe, n1, t, u, xn, high(u), ident)

            def qkv(t, u):
                pe.wait_ge(n1["xnT"], t + 1)
                wait(pe, s["ffn_added"], t - LANES + 1)
                self_qkv(pe, low(u), high(u), xnT[:, u], w_qkv).then_inc(s["qkv_filled"], 1)

            def turn_qk(t, u):
                pe.wait_ge(s["roped"], t + 1)
                pe.wait_ge(s["v_spread"], t + 1)
                for n in range(AG + 1):
                    mm = pe.transpose(ps[:, u, P * n:P * n + P], roped(u)[:, P * n:P * n + P], ident[:])
                mm.then_inc(s["qk_turned"], 1)

            def scores(t, u):
                pe.wait_ge(s["qt_ready"], t + 1)
                pe.wait_ge(s["kd_ready"], t + 1)
                for j in range(TB):
                    for a in range(2):
                        lo, at = 64 * a, 512 * a + P * j
                        mm = pe.matmul(ps[:, u, at:at + P], QT[lo:lo + 64, u, j], Kd(u)[lo:lo + 64, j],
                                       start=True, stop=True, tile_position=(lo, 0))
                mm.then_inc(s["s_filled"], 1)

            def turn_probs(t, u):
                pe.wait_ge(s["p_ready"], t + 1)
                for g in range(AKVH):
                    mm = pe.transpose(ps[:, u, P * g:P * g + P], probs(u)[:, P * g:P * g + P], ident[:])
                mm.then_inc(s["pt_filled"], 1)

            def values(t, u):
                pe.wait_ge(s["pt_ready"], t + 1)
                w = TB * (AD + 1)
                for g in range(AKVH):
                    at = 512 * (g // 4) + w * (g % 4)
                    mm = pe.matmul(ps[:, u, at:at + w], pT(u)[:, P * g:P * g + P], Vd[:, u, g], start=True, stop=True)
                mm.then_inc(s["av_filled"], 1)

            def turn_out(t, u):
                pe.wait_ge(s["o_ready"], t + 1)
                for j in range(TB):
                    mm = pe.transpose(high(u)[:, P * j:P * j + P], O(u)[:, P * j:P * j + P], ident[:])
                mm.then_inc(s["ot_filled"], 1)

            def project(t, u):
                pe.wait_ge(s["ot_ready"], t + 1)
                for r in range(AG):
                    mm = pe.matmul(low(u), OT(u)[:, r], w_o[:, r], start=(r == 0), stop=(r == AG - 1))
                mm.then_inc(s["proj_filled"], 1)

            def lora_down(t, u):
                pe.wait_ge(n2["xnT"], t + 1)
                for c in range(DC):
                    mm = pe.matmul(high(u)[0:NLR, 0:P], loraA[:, c], xnT[:, u, c], start=(c == 0), stop=(c == DC - 1))
                mm.then_inc(s["lora_filled"], 1)

            def ffn(t, u):
                for c in range(DC):
                    pe.matmul(low(u), xnT[:, u, c], w_ffn[:, c], start=(c == 0), stop=False)

            def lora_up(t, u):
                if isinstance(t, int) and t == 0:
                    pe.wait_ge(w_in, 32)
                    pe.wait_ge(zero_done, 5)
                pe.wait_ge(s["lora_ready"], t + 1)
                pe.matmul(low(u), lora_t[:, u], loraB[:], start=False, stop=True).then_inc(s["ffn_filled"], 1)

            over_lanes(pe, SLOTS0, STARTS0, {
                "turn1": after_first(first_turn), "qkv": after_first(qkv), "turn_qk": turn_qk, "scores": scores, "turn_probs": turn_probs,
                "values": values, "turn_out": turn_out, "project": project,
                "turn2": lambda t, u: norm_turn(pe, n2, t, u, xn, high(u), ident), "lora_down": lora_down, "ffn": ffn,
                "lora_up": lora_up, "turn3": lambda t, u: norm_turn(pe, n3, t, u, xn, high(u), ident)})

        @block.scalar
        def _(act):
            def evac_xnT(n):
                def stage(t, u):
                    act.wait_ge(n["xt"], t + 1)
                    act.activation(xnT[:, u].rearrange("p c q -> p (c q)"), high(u), ACT.Copy).then_inc(n["xnT"], 1)
                return stage

            def spread_v(t, u):
                if isinstance(t, int) and t < 2:
                    act.wait_ge(ones_done, TB * (t + 1))
                act.wait_ge(s["rope_terms"], t + 1)
                for j in range(TB):
                    rows = slice(L * j, L * j + L)
                    ins = act.activation(Vd[rows, u, :, j, 0:AD],
                                         high(u)[rows, AKV:2 * AKV].rearrange("p (g d) -> p g d", g=AKVH), ACT.Copy)
                ins.then_inc(s["v_spread"], 1)

            def evac_q(t, u):
                act.wait_ge(s["qk_turned"], t + 1)
                act.activation(QT[:, u].rearrange("p j (r q) -> p r j q", r=AG),
                               low(u).rearrange("p (r j q) -> p r j q", r=AG, j=TB), ACT.Copy).then_inc(s["qt_ready"], 1)

            def exps(t, u):
                act.wait_ge(s["s_shifted"], t + 1)
                for a in range(2):
                    ins = act.activation(probs(u)[:, 512 * a:512 * a + 512].rearrange("p (g j k) -> p j g k", g=4, j=TB),
                                         sm(u)[:, 512 * a:512 * a + 512].rearrange("p (j g k) -> p j g k", j=TB, g=4),
                                         ACT.Exp, scale=ASCALE)
                ins.then_inc(s["p_ready"], 1)

            def evac_pt(t, u):
                act.wait_ge(s["p_ready"], t + 1)
                act.wait_ge(s["pt_filled"], t + 1)
                act.activation(pT(u), ps[:, u, :], ACT.Copy).then_inc(s["pt_ready"], 1)

            def evac_ot(t, u):
                act.wait_ge(s["ot_filled"], t + 1)
                act.activation(OT(u).rearrange("p r (j q) -> p j r q", j=TB),
                               high(u).rearrange("p (j r q) -> p j r q", j=TB, r=AG), ACT.Copy).then_inc(s["ot_ready"], 1)

            def evac_pos(t, u):
                act.wait_ge(n3["xt"], t + 1)
                act.activation(posT[:, :, bass.ts(t, P)], high(u).rearrange("p (c n) -> p c n", c=DC), ACT.Copy)\
                    .then_inc(n3["xnT"], 1)

            over_lanes(act, SLOTS0, STARTS0, {"xnT1": after_first(evac_xnT(n1)), "spread_v": spread_v, "evac_q": evac_q, "exps": exps,
                                     "evac_pt": evac_pt, "evac_ot": evac_ot, "xnT2": evac_xnT(n2), "pos": evac_pos})

        @block.vector
        def _(dve):
            def stats(n, before):
                def stage(t, u):
                    tile_stats(dve, n, t, u, x_tile(t), small, gate, lambda: before(t))
                return stage

            def rows(n):
                return lambda t, u: norm_rows(dve, n, t, u, x_tile(t), small, xn)

            def rope(t, u):
                dve.wait_ge(s["qkv_filled"], t + 1)
                wait(dve, s["crucial_reduced"], t - LANES + 1)
                wait(dve, s["rest_reduced"], t - LANES + 1)
                src = ps[:, u, 0:QKH * AD].rearrange("p (n d) -> p n d", d=AD)
                half = AD // 2
                dve.tensor_tensor(terms(u).rearrange("p (n d) -> p n d", d=AD), src,
                                  cos[:].unsqueeze(1).to_broadcast([P, QKH, AD]), ALU.mult)
                dst = roped(u).rearrange("p (n d) -> p n d", d=AD)
                for h in range(2):
                    ins = dve.tensor_tensor(dst[:, :, half * h:half * h + half], src[:, :, half * (1 - h):half * (2 - h)],
                                            sin[:, half * h:half * h + half].unsqueeze(1).to_broadcast([P, QKH, half]),
                                            ALU.mult)
                ins.then_inc(s["rope_terms"], 1)

            def spread_k(t, u):
                dve.wait_ge(s["qk_turned"], t + 1)
                dve.tensor_tensor(Kd(u), high(u)[:, 0:P].rearrange("p (j k) -> p j k", j=TB).unsqueeze(2)
                                  .to_broadcast([P, TB, 4, L]),
                                  block16[:].unsqueeze(1).unsqueeze(3).to_broadcast([P, TB, 4, L]), ALU.mult)\
                    .then_inc(s["kd_ready"], 1)

            def mask_scores(t, u):
                dve.wait_ge(s["s_filled"], t + 1)
                v = sm(u).rearrange("p (n k) -> p n k", k=L)
                dve.tensor_tensor(v, ps[:, u, :].rearrange("p (n k) -> p n k", k=L),
                                  causal[:].unsqueeze(1).to_broadcast([P, 32, L]), ALU.add).then_inc(s["s_masked"], 1)
                dve.wait_ge(s["s_masked"], t + 1)
                dve.tensor_reduce(small["rmax"][:, u], v, AX.X, ALU.max).then_inc(s["max_done"], 1)

            def normalise(t, u):
                dve.wait_ge(s["av_filled"], t + 1)
                src = ps[:, u, :].rearrange("p (a n) -> p a n", a=2)[:, :, 0:4 * TB * (AD + 1)]\
                    .rearrange("p a (g j d) -> p a g j d", g=4, j=TB)
                rinv = small["rinv"][:, u].rearrange("p (a g j) -> p a g j", a=2, g=4)
                dve.reciprocal(rinv, src[:, :, :, :, AD]).then_inc(s["rinv_ready"], 1)
                dve.wait_ge(s["rinv_ready"], t + 1)
                dst = O(u).rearrange("p (j a g d) -> p a g j d", j=TB, a=2, g=4)
                for h in range(2):
                    ins = dve.tensor_tensor(dst[:, h], src[:, h, :, :, 0:AD],
                                            rinv[:, h].unsqueeze(3).to_broadcast([P, 4, TB, AD]), ALU.mult)
                ins.then_inc(s["o_ready"], 1)

            def add_projected(t, u):
                dve.wait_ge(s["proj_filled"], t + 1)
                dve.tensor_tensor(x_tile(t), x_tile(t), low(u), ALU.add).then_inc(s["proj_added"], 1)

            def lora_mask(t, u):
                dve.wait_ge(s["lora_filled"], t + 1)
                if isinstance(t, int) and t == 0:
                    dve.wait_ge(zero_done, 5)
                wait(dve, s["ffn_filled"], t - LANES + 1)
                dve.tensor_tensor(lora_t[0:NLR, u].rearrange("p (j q) -> p j q", j=TB),
                                  high(u)[0:NLR, 0:P].rearrange("p (j q) -> p j q", j=TB),
                                  adapter[:, bass.ts(t, TB)].unsqueeze(2).to_broadcast([NLR, TB, L]), ALU.mult)\
                    .then_inc(s["lora_ready"], 1)

            def add_ffn(t, u):
                dve.wait_ge(s["ffn_filled"], t + 1)
                dve.tensor_tensor(x_tile(t), x_tile(t), low(u), ALU.add).then_inc(s["ffn_added"], 1)

            def crucial_features(t, u):
                dve.wait_ge(n3["xnT"], t + 1)
                dve.tensor_tensor(crucial(u).rearrange("p (c n) -> p c n", c=DC), posT[:, :, bass.ts(t, P)],
                                  mask[:, :, bass.ts(t, P)], ALU.mult).then_inc(s["crucial_ready"], 1)

            def reduce_part(which, part, ready, done):
                def stage(t, u):
                    dve.wait_ge(s[ready], t + 1)
                    src = part(u).rearrange("p (c j n) -> p c j n", c=DC, j=TB)
                    for kind, op in ((0, ALU.max), (1, ALU.add)):
                        ins = dve.tensor_reduce(Y[:, :, kind, which, bass.ts(t, TB)], src, AX.X, op)
                    ins.then_inc(s[done], 1)
                return stage


            def before1(t):
                wait(dve, n3["xt"], t - LANES + 1)

            def before2(t):
                dve.wait_ge(s["proj_added"], t + 1)

            def before3(t):
                dve.wait_ge(s["ffn_added"], t + 1)

            over_lanes(dve, SLOTS0, STARTS0, {
                "stats1": after_first(stats(n1, before1)), "rows1": after_first(rows(n1)), "rope": rope, "spread_k": spread_k,
                "mask": mask_scores, "normalise": normalise, "add_proj": add_projected, "stats2": stats(n2, before2),
                "rows2": rows(n2), "lora_mask": lora_mask, "add_ffn": add_ffn, "stats3": stats(n3, before3),
                "rows3": rows(n3), "crucial": crucial_features, 
                "reduce_crucial": reduce_part(0, crucial, "crucial_ready", "crucial_reduced"),
                "reduce_rest": reduce_part(1, rest, "rest_ready", "rest_reduced")})


def mix_gates(nc, neghalf, ps, Y, ones, blend, band, affine, late, late_in):
    ctx = ExitStack()
    with ctx:
        def sb(name, shape, dt=F32):
            return ctx.enter_context(nc.sbuf_tensor(name, shape, dt))

        def sem(name):
            return ctx.enter_context(nc.semaphore(name))

        Z = sb("Z", [P, DC, 2, B])
        sq = sb("sq", [P, DC, 2, B])
        part = sb("part", [P, 2])
        moment = sb("moment", [P, 2])
        rstd = sb("mix_rstd", [P, 2])
        step, mean_step = sem("mix_step"), sem("mean_step")
        conv_done, sums_done, pow_done = sem("conv_done"), sem("sums_done"), sem("mix_pow_done")
        sig_done = sem("sig_done")
        conv = ps[:, 0, 0:DC * 2 * B]
        sums = ps[:, 1, 0:2]
        sums2 = ps[:, 2, 0:2]
        block = ctx.enter_context(nc.Block())
        count = float(B * D)
        by_which = "p c w b -> p w c b"

        @block.tensor
        def _(pe):
            pe.wait_ge(mean_step, 2)
            for o in range(DC):
                pairs = [(i, ch) for i in (o - 1, o, o + 1) if 0 <= i < DC for ch in range(2)]
                for n, (i, ch) in enumerate(pairs):
                    at = P * (o - i + 1)
                    mm = pe.matmul(conv[:, 2 * B * o:2 * B * (o + 1)], band[:, ch, at:at + P],
                                   Y[:, i, ch].rearrange("p w b -> p (w b)"), start=(n == 0), stop=(n == len(pairs) - 1))
            mm.then_inc(conv_done, 1)
            pe.wait_ge(step, 2)
            pe.matmul(sums, ones[:], part[:], start=True, stop=True).then_inc(sums_done, 1)
            pe.wait_ge(step, 6)
            pe.matmul(sums2, ones[:], part[:], start=True, stop=True).then_inc(sums_done, 1)

        @block.gpsimd
        def _(pool):
            pool.wait_ge(step, 7)
            for w in range(2):
                ins = pool.tensor_tensor(rstd[:, w:w + 1], moment[:, w:w + 1], neghalf[:], ALU.pow)
            ins.then_inc(pow_done, 1)

        @block.scalar
        def _(act):
            act.wait_ge(step, 9)
            act.activation(Z[:].rearrange("p c w b -> p (c w b)"), Z[:].rearrange("p c w b -> p (c w b)"),
                           ACT.Sigmoid).then_inc(sig_done, 1)

        @block.vector
        def _(dve):
            dve.tensor_scalar(Y[:, :, 1, 0, :], Y[:, :, 1, 0, :], 1.0 / L, float(L / TOPK), ALU.mult, ALU.mult)\
                .then_inc(mean_step, 1)
            dve.tensor_scalar(Y[:, :, 1, 1, :], Y[:, :, 1, 1, :], 1.0 / L, float(L / (L - TOPK)), ALU.mult, ALU.mult)\
                .then_inc(mean_step, 1)
            dve.wait_ge(late_in, 16 * LATE_LOADS)
            dve.tensor_tensor(late["w_ffn"][:], late["w_ffn"][:], late["ffn_mask"][:], ALU.mult)
            dve.wait_ge(conv_done, 1)
            z = Z[:].rearrange("p c w b -> p (c w b)")
            dve.tensor_copy(z, conv).then_inc(step, 1)
            dve.wait_ge(step, 1)
            dve.tensor_reduce(part[:], Z[:].rearrange(by_which), AX.XY, ALU.add).then_inc(step, 1)
            dve.wait_ge(sums_done, 1)
            dve.tensor_scalar(moment[:], sums, 1.0 / count, None, ALU.mult).then_inc(step, 1)
            dve.wait_ge(step, 3)
            dve.tensor_tensor(Z[:].rearrange("p c w b -> p c w b"), Z[:],
                              moment[:].unsqueeze(1).unsqueeze(3).to_broadcast([P, DC, 2, B]), ALU.subtract)\
                .then_inc(step, 1)
            dve.wait_ge(step, 4)
            dve.tensor_tensor(sq[:], Z[:], Z[:], ALU.mult).then_inc(step, 1)
            dve.wait_ge(step, 5)
            dve.tensor_reduce(part[:], sq[:].rearrange(by_which), AX.XY, ALU.add).then_inc(step, 1)
            dve.wait_ge(sums_done, 2)
            dve.tensor_scalar(moment[:], sums2, 1.0 / count, EPS, ALU.mult, ALU.add).then_inc(step, 1)
            dve.wait_ge(pow_done, 1)
            dve.tensor_tensor(Z[:], Z[:], rstd[:].unsqueeze(1).unsqueeze(3).to_broadcast([P, DC, 2, B]), ALU.mult)\
                .then_inc(mean_step, 1)
            dve.wait_ge(mean_step, 3)
            dve.tensor_scalar(z, z, affine[:, 0:1], affine[:, 1:2], ALU.mult, ALU.add).then_inc(step, 1)
            dve.wait_ge(step, 8)
            dve.tensor_scalar(z, z, 0.0, None, ALU.max).then_inc(step, 1)
            dve.wait_ge(sig_done, 1)
            dve.tensor_copy(blend[:, :, 0, :], Z[:, :, 1, :])
            dve.tensor_tensor(blend[:, :, 1, :], Z[:, :, 0, :], Z[:, :, 1, :], ALU.subtract)


def layer1(nc, a, X, mask, ident, neghalf, x_tile, ps, bufs, blend, late):
    posT, Y, lanes, xn, xnT, small, jmask, ones = bufs
    ctx = ExitStack()
    with ctx:
        def sb(name, shape, dt=F32):
            return ctx.enter_context(nc.sbuf_tensor(name, shape, dt))

        def sem(name):
            return ctx.enter_context(nc.semaphore(name))

        w_qkv, w_o, w_ffn, b_qk, b_v, b_o, keep = (
            late[k] for k in ("w_qkv", "w_o", "w_ffn", "b_qk", "b_v", "b_o", "keep"))
        QK = sb("lane_QK", [P, LANES, 4, P])
        V = sb("lane_V", [P, LANES, EW])
        p = sb("lane_p", [P, LANES, EW])
        gate = sb("gate1", [P, 1])

        n4, n5 = norm_sems(sem, "n4"), norm_sems(sem, "n5")
        names = ("gated", "gate_added", "mixed", "mix_turned", "mix_added", "bias_added", "qkv_filled", "v_ready",
                 "qk_ready", "kd_ready", "s_filled", "s_kept", "s_masked", "max_done", "s_shifted", "p_ready",
                 "sum_done", "rinv_ready", "pd_ready", "pt_filled", "pt_ready", "av_filled", "p_scaled",
                 "ot_ready", "proj_filled", "proj_added", "ffn_filled", "ffn_added")
        s = {k: sem(f"l1_{k}") for k in names}
        out_done = sem("out_done")

        mixed = lambda u: lanes[:, u, 0, 0:D]
        Kd = lambda u: lanes[:, u, 0].rearrange("p (a j h k) -> p a j h k", a=2, j=TB, h=4)
        Pd = lambda u: lanes[:, u, 0].rearrange("p (h j k) -> p h j k", h=EH, j=TB)
        pT = lambda u: lanes[:, u, 1]
        OT = lambda u: xnT[:, u, 0:EW // P]
        low = lambda u: ps[:, u, 0:512]
        high = lambda u: ps[:, u, 512:1024]

        block = ctx.enter_context(nc.Block())

        @block.sync
        def _(sp):
            def store(t, u):
                sp.wait_ge(s["ffn_added"], t + 1)
                if isinstance(t, int):
                    sp.dma_start(a["y"][t], x_tile(t)).then_inc(out_done, 16)
                else:
                    sp.dma_start(a["y"][bass.ds(t, 1)].rearrange("a p d -> (a p) d"), x_tile(t)).then_inc(out_done, 16)

            over_lanes(sp, SLOTS1, STARTS1, {"store": store})
            sp.wait_ge(out_done, 16 * NT)

        @block.gpsimd
        def _(pool):
            def bias_rows(t, u):
                pool.wait_ge(n4["xn"], t + 1)
                pool.tensor_tensor(x_tile(t), x_tile(t), b_o[:], ALU.add).then_inc(s["bias_added"], 1)

            def spread_k(t, u):
                pool.wait_ge(s["qk_ready"], t + 1)
                for half in range(2):
                    ins = pool.tensor_tensor(Kd(u)[:, half], QK[:, u, 2 + half].rearrange("p (j k) -> p j k", j=TB)
                                             .unsqueeze(2).to_broadcast([P, TB, 4, L]),
                                             jmask[:].unsqueeze(1).unsqueeze(3).to_broadcast([P, TB, 4, L]), ALU.mult)
                ins.then_inc(s["kd_ready"], 1)

            def shift(t, u):
                pool.wait_ge(s["max_done"], t + 1)
                v = p[:, u].rearrange("p (h k) -> p h k", h=EH)
                pool.tensor_tensor(v, v, small["rmax"][:, u, 0:EH].unsqueeze(2).to_broadcast([P, EH, L]), ALU.subtract)\
                    .then_inc(s["s_shifted"], 1)

            over_lanes(pool, SLOTS1, STARTS1, {
                "rstd1": lambda t, u: norm_rstd(pool, n4, t, u, small, neghalf),
                "bias": bias_rows, "spread_k": spread_k, "shift": shift,
                "rstd2": lambda t, u: norm_rstd(pool, n5, t, u, small, neghalf)})

        @block.tensor
        def _(pe):
            def turn_mix(t, u):
                pe.wait_ge(s["mixed"], t + 1)
                wait(pe, s["ffn_added"], t - LANES + 1)
                for c in range(DC):
                    mm = pe.transpose(low(u)[:, P * c:P * c + P], mixed(u)[:, P * c:P * c + P], ident[:])
                mm.then_inc(s["mix_turned"], 1)

            def qkv(t, u):
                pe.wait_ge(n4["xnT"], t + 1)
                for n in range(4):
                    for c in range(DC):
                        pe.matmul(low(u)[:, P * n:P * n + P], w_qkv[:, c, P * n:P * n + P], xnT[:, u, c],
                                  start=(c == 0), stop=(c == DC - 1))
                for c in range(DC):
                    mm = pe.matmul(high(u)[:, 0:EW], xnT[:, u, c], w_qkv[:, c, 2 * EW:], start=(c == 0), stop=(c == DC - 1))
                mm.then_inc(s["qkv_filled"], 1)

            def scores(t, u):
                pe.wait_ge(s["qk_ready"], t + 1)
                pe.wait_ge(s["kd_ready"], t + 1)
                for half in range(2):
                    for j in range(TB):
                        mm = pe.matmul(low(u)[L * j:L * j + L, P * half:P * half + P], QK[:, u, half, L * j:L * j + L],
                                       Kd(u)[:, half, j], start=True, stop=True, tile_position=(0, L * j))
                mm.then_inc(s["s_filled"], 1)

            def turn_probs(t, u):
                pe.wait_ge(s["pd_ready"], t + 1)
                pe.wait_ge(s["v_ready"], t + 1)
                for h in range(EH):
                    mm = pe.transpose(ps[:, u, P * h:P * h + P], Pd(u)[:, h].rearrange("p j k -> p (j k)"), ident[:])
                mm.then_inc(s["pt_filled"], 1)

            def values(t, u):
                pe.wait_ge(s["pt_ready"], t + 1)
                for h in range(EH):
                    n, at = h // 4, L * (h % 4)
                    mm = pe.matmul(high(u)[at:at + L, P * n:P * n + P], V[:, u, L * h:L * h + L],
                                   pT(u)[:, P * h:P * h + P], start=True, stop=True, tile_position=(0, at))
                mm.then_inc(s["av_filled"], 1)

            def project(t, u):
                pe.wait_ge(s["ot_ready"], t + 1)
                for n in range(EW // P):
                    mm = pe.matmul(low(u), OT(u)[:, n], w_o[:, n], start=(n == 0), stop=(n == EW // P - 1))
                mm.then_inc(s["proj_filled"], 1)

            def ffn(t, u):
                pe.wait_ge(n5["xnT"], t + 1)
                for c in range(DC):
                    mm = pe.matmul(low(u), xnT[:, u, c], w_ffn[:, c], start=(c == 0), stop=(c == DC - 1))
                mm.then_inc(s["ffn_filled"], 1)

            over_lanes(pe, SLOTS1, STARTS1, {
                "turn_mix": turn_mix, "turn1": lambda t, u: norm_turn(pe, n4, t, u, xn, high(u), ident), "qkv": qkv,
                "scores": scores, "turn_probs": turn_probs, "values": values, "project": project,
                "turn2": lambda t, u: norm_turn(pe, n5, t, u, xn, high(u), ident), "ffn": ffn})

        @block.scalar
        def _(act):
            def evac_xnT(n):
                def stage(t, u):
                    act.wait_ge(n["xt"], t + 1)
                    wait(act, s["ffn_filled"], t - LANES + 1)
                    act.activation(xnT[:, u].rearrange("p c q -> p (c q)"), high(u), ACT.Copy).then_inc(n["xnT"], 1)
                return stage

            def evac_qk(t, u):
                act.wait_ge(s["qkv_filled"], t + 1)
                wait(act, s["kd_ready"], t - LANES + 1)
                for n in range(4):
                    ins = act.activation(QK[:, u, n], low(u)[:, P * n:P * n + P], ACT.Identity, bias=b_qk[:, n:n + 1])
                ins.then_inc(s["qk_ready"], 1)

            def exps(t, u):
                act.wait_ge(s["s_shifted"], t + 1)
                act.activation(p[:, u], p[:, u], ACT.Exp).then_inc(s["p_ready"], 1)

            def evac_pt(t, u):
                act.wait_ge(s["pt_filled"], t + 1)
                wait(act, s["av_filled"], t - LANES + 1)
                act.activation(pT(u), ps[:, u, :], ACT.Copy).then_inc(s["pt_ready"], 1)

            def evac_ot(t, u):
                act.wait_ge(s["av_filled"], t + 1)
                act.activation(OT(u).rearrange("p n q -> p (n q)"), high(u)[:, 0:EW], ACT.Copy).then_inc(s["ot_ready"], 1)

            over_lanes(act, SLOTS1, STARTS1, {"xnT1": evac_xnT(n4), "evac_qk": evac_qk, "exps": exps, "evac_pt": evac_pt,
                                     "evac_ot": evac_ot, "xnT2": evac_xnT(n5)})

        @block.vector
        def _(dve):
            def gate_crucial(t, u):
                wait(dve, s["pt_filled"], t - LANES + 1)
                v = mixed(u).rearrange("p (c j n) -> p c j n", c=DC, j=TB)
                m = mask[:, :, bass.ts(t, P)].rearrange("p c (j n) -> p c j n", j=TB)
                dve.tensor_tensor(v, m, blend[:, :, 1, bass.ts(t, TB)].unsqueeze(3).to_broadcast([P, DC, TB, L]),
                                  ALU.mult).then_inc(s["gated"], 1)

            def add_rest(t, u):
                dve.wait_ge(s["gated"], t + 1)
                v = mixed(u).rearrange("p (c j n) -> p c j n", c=DC, j=TB)
                dve.tensor_tensor(v, v, blend[:, :, 0, bass.ts(t, TB)].unsqueeze(3).to_broadcast([P, DC, TB, L]),
                                  ALU.add).then_inc(s["gate_added"], 1)

            def mix(t, u):
                dve.wait_ge(s["gate_added"], t + 1)
                v = mixed(u).rearrange("p (c n) -> p c n", c=DC)
                dve.tensor_tensor(v, v, posT[:, :, bass.ts(t, P)], ALU.mult).then_inc(s["mixed"], 1)

            def add_mix(t, u):
                dve.wait_ge(s["mix_turned"], t + 1)
                dve.tensor_tensor(x_tile(t), x_tile(t), low(u), ALU.add).then_inc(s["mix_added"], 1)

            def before4(t):
                dve.wait_ge(s["mix_added"], t + 1)
                wait(dve, n5["xt"], t - LANES + 1)

            def before5(t):
                dve.wait_ge(s["proj_added"], t + 1)

            def stats(n, before):
                def stage(t, u):
                    tile_stats(dve, n, t, u, x_tile(t), small, gate, lambda: before(t))
                return stage

            def rows(n):
                return lambda t, u: norm_rows(dve, n, t, u, x_tile(t), small, xn)

            def evac_v(t, u):
                dve.wait_ge(s["qkv_filled"], t + 1)
                wait(dve, s["av_filled"], t - LANES + 1)
                dve.tensor_tensor(V[:, u], high(u)[:, 0:EW], b_v[:], ALU.add).then_inc(s["v_ready"], 1)

            def mask_scores(t, u):
                dve.wait_ge(s["s_filled"], t + 1)
                v = p[:, u].rearrange("p (h k) -> p h k", h=EH)
                dve.tensor_tensor(v, low(u)[:, 0:EW].rearrange("p (h k) -> p h k", h=EH),
                                  keep[:, 0].unsqueeze(1).to_broadcast([P, EH, L]), ALU.mult).then_inc(s["s_kept"], 1)
                dve.wait_ge(s["s_kept"], t + 1)
                dve.tensor_tensor(v, v, keep[:, 1].unsqueeze(1).to_broadcast([P, EH, L]), ALU.add).then_inc(s["s_masked"], 1)
                dve.wait_ge(s["s_masked"], t + 1)
                dve.tensor_reduce(small["rmax"][:, u, 0:EH], v, AX.X, ALU.max).then_inc(s["max_done"], 1)

            def spread_p(t, u):
                dve.wait_ge(s["p_ready"], t + 1)
                v = p[:, u].rearrange("p (h k) -> p h k", h=EH)
                dve.tensor_reduce(small["rsum"][:, u], v, AX.X, ALU.add).then_inc(s["sum_done"], 1)
                dve.wait_ge(s["sum_done"], t + 1)
                dve.reciprocal(small["rinv"][:, u, 0:EH], small["rsum"][:, u]).then_inc(s["rinv_ready"], 1)
                dve.wait_ge(s["rinv_ready"], t + 1)
                dve.tensor_tensor(v, v, small["rinv"][:, u, 0:EH].unsqueeze(2).to_broadcast([P, EH, L]), ALU.mult)\
                    .then_inc(s["p_scaled"], 1)
                dve.wait_ge(s["p_scaled"], t + 1)
                for j in range(TB):
                    ins = dve.tensor_scalar(Pd(u)[:, :, j], v, jmask[:, j:j + 1], None, ALU.mult)
                ins.then_inc(s["pd_ready"], 1)

            def add_projected(t, u):
                dve.wait_ge(s["proj_filled"], t + 1)
                dve.wait_ge(s["bias_added"], t + 1)
                dve.tensor_tensor(x_tile(t), x_tile(t), low(u), ALU.add).then_inc(s["proj_added"], 1)

            def add_ffn(t, u):
                dve.wait_ge(s["ffn_filled"], t + 1)
                dve.tensor_tensor(x_tile(t), x_tile(t), low(u), ALU.add).then_inc(s["ffn_added"], 1)

            over_lanes(dve, SLOTS1, STARTS1, {
                "gate": gate_crucial, "add_rest": add_rest, "mix": mix, "add_mix": add_mix, "stats1": stats(n4, before4), "rows1": rows(n4),
                "evac_v": evac_v, "mask": mask_scores, "spread_p": spread_p,
                "add_proj": add_projected, "stats2": stats(n5, before5), "rows2": rows(n5), "add_ffn": add_ffn})


def k_perm():
    return np.concatenate([np.arange(h * HD + lo, h * HD + hi) for h, lo, hi in K_ROWS])


def by_chunks(w):
    return np.ascontiguousarray(w.T.reshape(-1, P, w.shape[0]).transpose(1, 0, 2))


def tables():
    rows = np.arange(P)
    q = rows % L
    freqs = (1.0 / 10000.0 ** (np.arange(0, AD, 2, dtype=np.float32) / np.float32(AD))).astype(np.float32)
    ang = np.outer(q.astype(np.float32), freqs).astype(np.float32)
    cos, sin = np.cos(ang), np.sin(ang)
    later = np.arange(L)[None, :] > q[:, None]
    out = {
        "ident": np.eye(P), "cos": np.concatenate([cos, cos], 1), "sin": np.concatenate([-sin, sin], 1),
        "causal": np.where(later, -1e30, 0.0), "keep1": np.where(later, 0.0, 1.0), "masked1": np.where(later, -10000.0, 0.0),
        "block16": rows[:, None] // AD % 4 == np.arange(4)[None, :], "jmask": rows[:, None] // L == np.arange(TB)[None, :],
        "batches": np.broadcast_to(np.arange(B)[None, :], (NLR, B)), "chosen": (np.arange(NLR)[:, None] // 16) + 2,
        "shifted": np.arange(3 * P + TAPS - 1)[None, :] == rows[:, None] + P + TAPS // 2,
    }
    return {k: np.ascontiguousarray(v.astype(np.float32)) for k, v in out.items()}


def lay_out(x, ctx_4096, L0_xattn_Wq, L0_xattn_Wk, L0_xattn_Wv, L0_xattn_Wo, L0_attn_wq, L0_attn_wk, L0_attn_wv,
            L0_attn_wo, L0_ffn_weight, L0_ffn_bias, L0_ffn_lora_A, L0_ffn_lora_B, L0_ffn_lora_start_indices,
            L1_xattn_conv_w, L1_xattn_bn_gamma, L1_xattn_bn_beta, L1_attn_w_qkv, L1_attn_b_qkv, L1_attn_w_o,
            L1_attn_b_o, L1_ffn_W, L1_ffn_mask):
    perm = k_perm()
    c = np.ascontiguousarray
    out = {}
    out["x"] = c(x.reshape(NT, P, D).transpose(1, 0, 2))
    out["ctxT"] = c(ctx_4096.reshape(B, CTX, DC, P).transpose(0, 3, 2, 1))
    out["ctx_last"] = c(ctx_4096[:, CTX - 1, :].reshape(B, DC, P).transpose(2, 1, 0))
    heads, inner = perm // HD, perm % HD
    q_rows = np.concatenate([((heads[P * k:P * k + P] * G + r) * HD + inner[P * k:P * k + P])
                             for k in range(NKT) for r in range(G)])
    out["WqT"] = by_chunks(L0_xattn_Wq[q_rows])
    out["WkT"] = by_chunks(L0_xattn_Wk[perm])
    out["WvT"] = by_chunks(L0_xattn_Wv)
    col = np.arange(KW)
    o_cols = np.concatenate([((col[P * k:P * k + P] // HD) * G + r) * HD + col[P * k:P * k + P] % HD
                             for k in range(NKT) for r in range(G)])
    out["WoT"] = c(L0_xattn_Wo[:, o_cols].T.reshape(NKT * G, P, D).transpose(1, 0, 2))
    halves = np.concatenate([np.arange(0, AD, 2), np.arange(1, AD, 2)])
    k_cols = (np.arange(AKVH)[:, None] * AD + halves[None, :]).ravel()
    q_cols = np.concatenate([((np.arange(AKVH) * AG + r)[:, None] * AD + halves[None, :]).ravel() for r in range(AG)])
    out["w_qkv0"] = by_chunks(np.concatenate([L0_attn_wq[:, q_cols], L0_attn_wk[:, k_cols], L0_attn_wv], 1).T)
    o_rows = np.stack([((np.arange(AKVH) * AG + r)[:, None] * AD + np.arange(AD)[None, :]).ravel() for r in range(AG)])
    out["w_o0"] = c(L0_attn_wo[o_rows].transpose(1, 0, 2))
    out["w_ffn0"] = by_chunks(L0_ffn_weight)
    out["ffn_bias"] = c(L0_ffn_bias)
    out["loraA"] = by_chunks(L0_ffn_lora_A.reshape(NLR, D))
    out["loraB"] = c(L0_ffn_lora_B.transpose(0, 2, 1).reshape(NLR, D))
    out["starts"] = c(L0_ffn_lora_start_indices)
    out["taps"] = c(L1_xattn_conv_w.reshape(-1))
    out["bn_gamma"] = c(L1_xattn_bn_gamma)
    out["bn_beta"] = c(L1_xattn_bn_beta)
    out["w_qkv1"] = by_chunks(L1_attn_w_qkv)
    out["b_qk1"] = c(L1_attn_b_qkv[0:2 * EW].reshape(-1, P).T)
    out["b_v1"] = c(L1_attn_b_qkv[2 * EW:])
    out["w_o1"] = by_chunks(L1_attn_w_o)
    out["b_o1"] = c(L1_attn_b_o)
    out["w_ffn1"] = by_chunks(L1_ffn_W)
    out["ffn_mask"] = by_chunks(L1_ffn_mask)
    out.update(tables())
    return out


def kernel(**inputs):
    import concourse.bacc as bacc
    from concourse.bass_utils import run_bass_kernel_spmd

    nc = bacc.Bacc("TRN2", target_bir_lowering=False, num_devices=1)
    arrays = lay_out(**{k: np.asarray(v) for k, v in inputs.items()})
    a = {k: nc.dram_tensor(f"in_{k}", v.shape, mybir.dt.from_np(v.dtype), kind="ExternalInput").ap()
         for k, v in arrays.items()}
    a["y"] = nc.dram_tensor("y", (NT, P, D), F32, kind="ExternalOutput").ap()
    build_program(nc, a)
    r = run_bass_kernel_spmd(nc, [{f"in_{k}": v for k, v in arrays.items()}], core_ids=[0])
    return r.results[0]["y"].reshape(B, L, D)
```
